# Optimizing a Trainium2 kernel written in Bass

```python
import numpy as np
import jax
import jax.numpy as jnp

def _softmax(x, axis=-1):
    return jax.nn.softmax(x, axis=axis)

def _gelu(x):
    return jax.nn.gelu(x, approximate=True)

def _silu(x):
    return jax.nn.silu(x)

def _sigmoid(x):
    return jax.nn.sigmoid(x)

def _layernorm(x, axis=-1, eps=1e-05):
    m = jnp.mean(x, axis=axis, keepdims=True)
    v = jnp.var(x, axis=axis, keepdims=True)
    return (x - m) / jnp.sqrt(v + eps)

def _scatter_add(tgt, idx, src, axis=0):
    return tgt.at[idx].add(src)

def _segment_sum(src, seg, n):
    return jax.ops.segment_sum(src, seg, n)
kernel_name = 'mk_conv_preact_d2_conv_nchw384_r4_f1eb52'

def setup_inputs(seed: int=0):
    np.random.seed(seed)
    _w = jnp.asarray

    def _rec_inputs():
        import jax
        import jax.numpy as jnp
        _gk = jax.random.key(seed)
        x = -0.0001476 + 0.9999 * jax.random.normal(jax.random.fold_in(_gk, 1), (32, 96, 56, 56), jnp.float32)
        return x
    x = _rec_inputs()

    def _L0_conv_setup():
        import jax, jax.numpy as jnp
        import numpy as np
        DIM = 96
        KERNEL = 31
        PAD = KERNEL // 2
        key = jax.random.key(seed)
        k1, k2 = jax.random.split(key)
        x = jax.random.normal(k1, (32, DIM, 56, 56), dtype=jnp.float32)
        weight = jax.random.normal(k2, (DIM, 1, KERNEL, KERNEL), dtype=jnp.float32)
        bias_term = jnp.zeros((DIM,), dtype=jnp.float32)
        return {'x': x, 'weight': weight, 'bias_term': bias_term}
    _L0_conv_all = _L0_conv_setup()
    _L0_conv_in = {k: v for k, v in _L0_conv_all.items() if k in ('weight', 'bias_term')}
    del _L0_conv_all

    def _L1_conv_setup():
        import jax, jax.numpy as jnp
        import numpy as np
        GH, GW = (7, 7)
        SH, SW = (3, 3)
        D, NHEADS, MLP = (96, 12, 384)
        EPS = 1e-06

        def _ln(x, s, b):
            m = jnp.mean(x, axis=-1, keepdims=True)
            v = jnp.var(x, axis=-1, keepdims=True)
            return (x - m) * jax.lax.rsqrt(v + EPS) * s + b

        def _vit(t, ln1_s, ln1_b, wq, bq, wk, bk, wv, bv, wo, bo, ln2_s, ln2_b, w1, b1, w2, b2):
            N, S, _ = t.shape
            dh = D // NHEADS
            h = _ln(t, ln1_s, ln1_b)
            q = (h @ wq + bq).reshape(N, S, NHEADS, dh)
            k = (h @ wk + bk).reshape(N, S, NHEADS, dh)
            v = (h @ wv + bv).reshape(N, S, NHEADS, dh)
            scores = jnp.einsum('nqhd,nkhd->nhqk', q, k) / np.sqrt(dh)
            attn = jax.nn.softmax(scores, axis=-1)
            o = jnp.einsum('nhqk,nkhd->nqhd', attn, v).reshape(N, S, D)
            t = t + o @ wo + bo
            h = _ln(t, ln2_s, ln2_b)
            t = t + jax.nn.gelu(h @ w1 + b1) @ w2 + b2
            return t
        key = jax.random.key(seed)
        ks = jax.random.split(key, 12)
        sd = 1.0 / np.sqrt(D)
        x = jax.random.normal(ks[0], (32, D, 56, 56), dtype=jnp.float32)
        return {'x': x, 'ln1_s': jnp.ones((D,), jnp.float32), 'ln1_b': jnp.zeros((D,), jnp.float32), 'wq': jax.random.normal(ks[1], (D, D), jnp.float32) * sd, 'bq': jnp.zeros((D,), jnp.float32), 'wk': jax.random.normal(ks[2], (D, D), jnp.float32) * sd, 'bk': jnp.zeros((D,), jnp.float32), 'wv': jax.random.normal(ks[3], (D, D), jnp.float32) * sd, 'bv': jnp.zeros((D,), jnp.float32), 'wo': jax.random.normal(ks[4], (D, D), jnp.float32) * sd, 'bo': jnp.zeros((D,), jnp.float32), 'ln2_s': jnp.ones((D,), jnp.float32), 'ln2_b': jnp.zeros((D,), jnp.float32), 'w1': jax.random.normal(ks[5], (D, MLP), jnp.float32) * sd, 'b1': jnp.zeros((MLP,), jnp.float32), 'w2': jax.random.normal(ks[6], (MLP, D), jnp.float32) / np.sqrt(MLP), 'b2': jnp.zeros((D,), jnp.float32)}
    _L1_conv_all = _L1_conv_setup()
    _L1_conv_in = {k: v for k, v in _L1_conv_all.items() if k in ('ln1_s', 'ln1_b', 'wq', 'bq', 'wk', 'bk', 'wv', 'bv', 'wo', 'bo', 'ln2_s', 'ln2_b', 'w1', 'b1', 'w2', 'b2')}
    del _L1_conv_all
    return {'x': x, 'L0_conv_weight': _L0_conv_in['weight'], 'L0_conv_bias_term': _L0_conv_in['bias_term'], 'L1_conv_ln1_s': _L1_conv_in['ln1_s'], 'L1_conv_ln1_b': _L1_conv_in['ln1_b'], 'L1_conv_wq': _L1_conv_in['wq'], 'L1_conv_bq': _L1_conv_in['bq'], 'L1_conv_wk': _L1_conv_in['wk'], 'L1_conv_bk': _L1_conv_in['bk'], 'L1_conv_wv': _L1_conv_in['wv'], 'L1_conv_bv': _L1_conv_in['bv'], 'L1_conv_wo': _L1_conv_in['wo'], 'L1_conv_bo': _L1_conv_in['bo'], 'L1_conv_ln2_s': _L1_conv_in['ln2_s'], 'L1_conv_ln2_b': _L1_conv_in['ln2_b'], 'L1_conv_w1': _L1_conv_in['w1'], 'L1_conv_b1': _L1_conv_in['b1'], 'L1_conv_w2': _L1_conv_in['w2'], 'L1_conv_b2': _L1_conv_in['b2']}

def reference(x, L0_conv_weight, L0_conv_bias_term, L1_conv_ln1_s, L1_conv_ln1_b, L1_conv_wq, L1_conv_bq, L1_conv_wk, L1_conv_bk, L1_conv_wv, L1_conv_bv, L1_conv_wo, L1_conv_bo, L1_conv_ln2_s, L1_conv_ln2_b, L1_conv_w1, L1_conv_b1, L1_conv_w2, L1_conv_b2):
    import jax
    import jax.numpy as jnp

    def _L0_conv_ref(x, weight, bias_term):
        import jax, jax.numpy as jnp
        import numpy as np
        DIM = 96
        KERNEL = 31
        PAD = KERNEL // 2
        out = jax.lax.conv_general_dilated(x, weight, window_strides=(1, 1), padding=[(PAD, PAD), (PAD, PAD)], dimension_numbers=('NCHW', 'OIHW', 'NCHW'), feature_group_count=DIM)
        return out + bias_term[None, :, None, None]

    def _L1_conv_ref(x, ln1_s, ln1_b, wq, bq, wk, bk, wv, bv, wo, bo, ln2_s, ln2_b, w1, b1, w2, b2):
        import jax, jax.numpy as jnp
        import numpy as np
        GH, GW = (7, 7)
        SH, SW = (3, 3)
        D, NHEADS, MLP = (96, 12, 384)
        EPS = 1e-06

        def _ln(x, s, b):
            m = jnp.mean(x, axis=-1, keepdims=True)
            v = jnp.var(x, axis=-1, keepdims=True)
            return (x - m) * jax.lax.rsqrt(v + EPS) * s + b

        def _vit(t, ln1_s, ln1_b, wq, bq, wk, bk, wv, bv, wo, bo, ln2_s, ln2_b, w1, b1, w2, b2):
            N, S, _ = t.shape
            dh = D // NHEADS
            h = _ln(t, ln1_s, ln1_b)
            q = (h @ wq + bq).reshape(N, S, NHEADS, dh)
            k = (h @ wk + bk).reshape(N, S, NHEADS, dh)
            v = (h @ wv + bv).reshape(N, S, NHEADS, dh)
            scores = jnp.einsum('nqhd,nkhd->nhqk', q, k) / np.sqrt(dh)
            attn = jax.nn.softmax(scores, axis=-1)
            o = jnp.einsum('nhqk,nkhd->nqhd', attn, v).reshape(N, S, D)
            t = t + o @ wo + bo
            h = _ln(t, ln2_s, ln2_b)
            t = t + jax.nn.gelu(h @ w1 + b1) @ w2 + b2
            return t
        B, C, H, W = x.shape
        nh, nw = (H // GH, W // GW)
        xs = jnp.roll(x, (-SH, -SW), axis=(2, 3))
        t = xs.reshape(B, C, nh, GH, nw, GW).transpose(0, 2, 4, 3, 5, 1).reshape(B * nh * nw, GH * GW, C)
        t = _vit(t, ln1_s, ln1_b, wq, bq, wk, bk, wv, bv, wo, bo, ln2_s, ln2_b, w1, b1, w2, b2)
        y = t.reshape(B, nh, nw, GH, GW, C).transpose(0, 5, 1, 3, 2, 4).reshape(B, C, H, W)
        return jnp.roll(y, (SH, SW), axis=(2, 3))

    def _gn(v, G=32, eps=1e-05):
        B_, C_, H_, W_ = v.shape
        g = v.reshape(B_, G, C_ // G, H_, W_)
        m = jnp.mean(g, axis=(2, 3, 4), keepdims=True)
        s = jnp.var(g, axis=(2, 3, 4), keepdims=True)
        return ((g - m) / jnp.sqrt(s + eps)).reshape(v.shape)

    def _ln_c(v, eps=1e-06):
        m = jnp.mean(v, axis=1, keepdims=True)
        s = jnp.var(v, axis=1, keepdims=True)
        return (v - m) / jnp.sqrt(s + eps)

    def _ln_t(v, eps=1e-05):
        m = jnp.mean(v, axis=-1, keepdims=True)
        s = jnp.var(v, axis=-1, keepdims=True)
        return (v - m) / jnp.sqrt(s + eps)

    def _to_tokens(v):
        B_, C_, H_, W_ = v.shape
        return v.reshape(B_, C_, H_ * W_).transpose(0, 2, 1)

    def _from_tokens(t, like):
        B_, C_, H_, W_ = like.shape
        return t.transpose(0, 2, 1).reshape(B_, C_, H_, W_)
    x = x + _L0_conv_ref(_gn(x), L0_conv_weight, L0_conv_bias_term)
    x = x + _L1_conv_ref(_gn(x), L1_conv_ln1_s, L1_conv_ln1_b, L1_conv_wq, L1_conv_bq, L1_conv_wk, L1_conv_bk, L1_conv_wv, L1_conv_bv, L1_conv_wo, L1_conv_bo, L1_conv_ln2_s, L1_conv_ln2_b, L1_conv_w1, L1_conv_b1, L1_conv_w2, L1_conv_b2)
    return x

_drawn_inputs = setup_inputs


def setup_inputs(seed=0):
    import zlib

    import numpy as np

    out = dict(_drawn_inputs(seed))
    spreads = {'L0_conv_bias_term': (0.0, 0.8),
     'L1_conv_ln1_s': (1.0, 0.6),
     'L1_conv_ln1_b': (0.0, 0.8),
     'L1_conv_bq': (0.0, 0.8),
     'L1_conv_bk': (0.0, 2.0),
     'L1_conv_bv': (0.0, 0.8),
     'L1_conv_bo': (0.0, 2.0),
     'L1_conv_ln2_s': (1.0, 0.6),
     'L1_conv_ln2_b': (0.0, 2.0),
     'L1_conv_b1': (0.0, 2.0),
     'L1_conv_b2': (0.0, 2.0)}
    factors = {'L1_conv_wq': 5.124, 'L1_conv_wk': 5.048, 'L1_conv_wv': 4.19, 'L1_conv_wo': 3.863}
    for name, (base, spread) in spreads.items():
        noise = np.random.default_rng([zlib.crc32(name.encode()), seed]).standard_normal(out[name].shape)
        drawn = base * np.exp(spread * noise) if base else spread * noise
        out[name] = jnp.asarray(drawn.astype(out[name].dtype))
    for name, factor in factors.items():
        out[name] = (out[name] * factor).astype(out[name].dtype)
    return out
```

```python
from contextlib import ExitStack

import numpy as np
import concourse.bass as bass
from concourse import mybir

F32 = mybir.dt.float32
ALU = mybir.AluOpType
ACT = mybir.ActivationFunctionType
AX = mybir.AxisListType

P = 128
BATCH, C, HW = 32, 96, 56
NPIX = HW * HW
KS, PAD = 31, 15
GROUPS, GC = 32, 3
BR, BC = 16, 8
NYB, NXB = 4, 7
ROWS_LAST = HW - (NYB - 1) * BR
STRIPE = BR * HW
STRIPE_LAST = ROWS_LAST * HW
PITCH = KS + BC
WROWS = KS + 2 * BR
WLEN = WROWS * PITCH + 2 * BC
TLEN = (3 * BR - 1) * PITCH + 5 * BC
WIN, NWIN = 7, 8
SHIFT = 3
TOK = WIN * WIN
NT = NWIN * TOK
HEADS, DH, MLP = 12, 8, 384
QG, HPG = 2, 6
QR = P // QG
GRP = HPG * DH
NM = MLP // P
PAIRS = NWIN // 2
WS = 64
XW = HW + SHIFT
VA = DH + 1
MAXCOL = GRP

CONST = {}
_n = 0
for _name, _w in (("ident", P), ("samebatch", P), ("batchsum", BATCH), ("headmask", HPG),
                  ("center", C), ("average", C), ("samegroup", C), ("onesrows", 1)):
    CONST[_name] = (_n, _n + _w)
    _n += _w
NCONST = _n


def constants():
    t = np.zeros((P, NCONST), np.float32)
    p = np.arange(P)

    def put(name, a):
        lo, hi = CONST[name]
        t[:a.shape[0], lo:hi] = a
    put("ident", np.eye(P))
    n_group = GC * NPIX
    put("samebatch", (p[:, None] % BATCH == p[None] % BATCH) / n_group)
    put("batchsum", (p[:, None] % BATCH == np.arange(BATCH)[None]) / n_group)
    r = p % QR
    put("headmask", np.stack([(r // DH == j) & (r < GRP) | (r == MAXCOL + j) for j in range(HPG)], 1) * 1.0)
    put("center", np.eye(C) - 1.0 / C)
    put("average", np.full((C, C), 1.0 / C))
    put("onesrows", ((r >= MAXCOL) & (r < MAXCOL + HPG))[:, None] * 1.0)
    return t


def conv_pass(nc, x, weight, conv_bias, const, wpad, x1, gn2):
    B = 4
    NIT = GROUPS // B
    XR = 4
    with ExitStack() as ctx:
        def sb(name, shape):
            return ctx.enter_context(nc.sbuf_tensor(name, shape, F32))

        def sem(name):
            return ctx.enter_context(nc.semaphore(name))

        cst = sb("a_const", [P, NCONST])
        xin = sb("xin", [P, XR, GC, STRIPE])
        xn = sb("xn", [P, 2, GC, NXB, BR * BC])
        x1t = sb("x1t", [P, 2, GC, STRIPE])
        blocks = sb("blocks", [P, 2, NXB, (NYB + 2) * BATCH])
        toep = sb("toep", [P, 3, TLEN])
        junk = sb("junk", [P, GC, STRIPE])
        sums = sb("sums", [P, 2, 2])
        mom = sb("mom", [P, 2, 4])
        aff = sb("aff", [P, 2, 2])
        sums1 = sb("sums1", [P, 2, GROUPS])
        sums1c = sb("sums1c", [P, 2, C])
        mom1 = sb("mom1", [C, 4, BATCH])
        biasb = sb("biasb", [P, C])
        eps = sb("a_eps", [P, 1])
        wst = sb("wst", [C, KS * KS])
        wpd = sb("wpd", [C, WLEN])
        ps_conv = ctx.enter_context(nc.psum_tensor("ps_conv", [P, 4, 512], F32))
        ps_tr = ctx.enter_context(nc.psum_tensor("ps_tr", [P, 4, 512], F32))

        x_loaded = [sem(f"x_loaded{r}") for r in range(XR)]
        t_loaded = [sem(f"t_loaded{r}") for r in range(3)]
        x1_stored = [sem(f"x1_stored{r}") for r in range(2)]
        const_loaded, w_loaded, w_padded, wpad_stored = (sem(n) for n in ("const_loaded", "w_loaded", "w_padded",
                                                                          "wpad_stored"))
        zeroed, eps_set, xn_zeroed = sem("zeroed"), sem("eps_set"), sem("xn_zeroed")
        var_tmp, fin_w = sem("var_tmp"), sem("fin_w")
        summed = sem("summed")
        sums_done, moments, var_done, log_done, std_done, affine = (sem(n) for n in (
            "sums_done", "moments", "var_done", "log_done", "std_done", "affine"))
        normed, tin_ps, tin_done, conv_ps, x1_done, x1_cleared, sums1_done = (sem(n) for n in (
            "normed", "tin_ps", "tin_done", "conv_ps", "x1_done", "x1_cleared",
            "sums1_done"))
        fin_v, fin_p, fin_a = sem("fin_v"), sem("fin_p"), sem("fin_a")

        def cc(name, rows=P):
            lo, hi = CONST[name]
            return cst[0:rows, lo:hi]

        def steps(eng, step):
            for s in range(B):
                step(0, s)
            with eng.Fori(1, NIT, 1) as i:
                for s in range(B):
                    step(i, s)
            for s in range(2):
                step(NIT, s)

        def ok(i, k, n):
            if isinstance(i, int):
                return 0 <= n * i + k < n * NIT
            return True

        def dram_rows(t, ch, last):
            src = t[:, bass.ds(ch, 1), :, :].rearrange("b c h w -> b (c h w)")
            if last:
                return src[:, (NYB - 1) * STRIPE:]
            return src[:, 0:(NYB - 1) * STRIPE].rearrange("b (y s) -> y b s", y=NYB - 1)

        def settled(pool):
            pool.nop(nofuse=True)

        block = ctx.enter_context(nc.Block())

        @block.sync
        def _(sp):
            sp.dma_start(cst[:, :], const).then_inc(const_loaded, 16)
            sp.dma_start(biasb[:, :], conv_bias.rearrange("(a c) -> a c", a=1).broadcast_to((P, C))).then_inc(
                const_loaded, 16)
            sp.dma_start(wst[:, :], weight.rearrange("c a h w -> c (a h w)")).then_inc(w_loaded, 16)
            sp.wait_ge(w_padded, 1)
            sp.dma_start(wpad, wpd[:, :]).then_inc(wpad_stored, 16)
            sp.wait_ge(wpad_stored, 16)

            def step(i, s):
                if ok(i, s, B):
                    if not isinstance(i, int) or i:
                        sp.wait_ge(x1_done, 3 * (B * i + s) - 3 * XR + 3)
                    for ch in range(GC):
                        c = GC * (B * i + s) + ch
                        sp.dma_start(xin[0:96, s, ch, :], dram_rows(x, c, False)).then_inc(x_loaded[s], 16)
                        sp.dma_start(xin[96:P, s, ch, 0:STRIPE_LAST], dram_rows(x, c, True)).then_inc(
                            x_loaded[s], 16)
                if ok(i, s - 1, B):
                    for ch in range(GC):
                        c = GC * (B * i + s - 1) + ch
                        if not (isinstance(i, int) and c < 3):
                            sp.wait_ge(conv_ps, c - 2)
                        src = wpad[bass.ds(c, 1), :]
                        src = bass.AP(src.tensor, src.offset, [[PITCH, BR], [1, BC], [1, TLEN]])
                        sp.dma_start(toep[:, ch, 0:TLEN], src).then_inc(t_loaded[ch], 16)
            steps(sp, step)

        @block.gpsimd
        def _(pool):
            pool.memset(wpd[:, :], 0.0).then_inc(zeroed, 1)
            for r in range(2):
                for e in (0, NYB + 1):
                    ins = pool.memset(blocks[:, r, :, e * BATCH:(e + 1) * BATCH], 0.0)
            ins.then_inc(xn_zeroed, 1)
            pool.wait_ge(xn_zeroed, 1)
            pool.memset(xin[96:P, :, :, STRIPE_LAST:], 0.0)
            pool.memset(xn[96:P, :, :, :, ROWS_LAST * BC:], 0.0).then_inc(xn_zeroed, 1)

            def step(i, s):
                if ok(i, s, B):
                    g = B * i + s
                    pool.wait_ge(affine, g + 1)
                    if not (isinstance(i, int) and g < 2):
                        pool.wait_ge(tin_ps, 3 * g - 3)
                    settled(pool)
                    for ch in range(GC):
                        for r, n in ((slice(0, 96), BR), (slice(96, P), ROWS_LAST)):
                            src = xin[r, s, ch, 0:n * HW].rearrange("p (y b c) -> p y b c", y=n, b=NXB)
                            dst = xn[r, s % 2, ch, :, 0:n * BC].rearrange("p b (y c) -> p y b c", y=n)
                            ins = pool.tensor_scalar(dst, src, aff[r, s % 2, 0:1], aff[r, s % 2, 1:2], ALU.mult,
                                                     ALU.add)
                    ins.then_inc(normed, 1)
                if ok(i, s - 2, B):
                    g = B * i + s - 2
                    pool.wait_ge(x1_done, 3 * g + 3)
                    settled(pool)
                    pool.memset(x1t[96:P, s % 2, :, STRIPE_LAST:], 0.0).then_inc(x1_cleared, 1)
                    for ch in range(GC):
                        c = GC * g + ch
                        pool.dma_start(dram_rows(x1, c, False), x1t[0:96, s % 2, ch, :]).then_inc(
                            x1_stored[s % 2], 16)
                        pool.dma_start(dram_rows(x1, c, True), x1t[96:P, s % 2, ch, 0:STRIPE_LAST]).then_inc(
                            x1_stored[s % 2], 16)
            steps(pool, step)
            for r in range(2):
                pool.wait_ge(x1_stored[r], 96 * (GROUPS // 2))

        @block.scalar
        def _(act):
            act.wait_ge(xn_zeroed, 2)
            act.wait_ge(eps_set, 1)

            def stats(i, before, src, dst, done):
                if not isinstance(i, int) or before:
                    act.wait_ge(summed, before)
                act.activation(junk[:, :, :], src, ACT.Copy, accum_out=dst[0]).then_inc(summed, 1)
                act.wait_ge(summed, before + 1)
                act.activation(junk[:, :, :], src, ACT.Square, accum_out=dst[1]).then_inc(summed, 1)
                act.wait_ge(summed, before + 2)
                act.nop().then_inc(done, 1)

            def groups_before(i, s, off):
                n = B * i + s - off
                return min(max(n, 0), GROUPS) if isinstance(i, int) else n

            def step(i, s):
                g = B * i + s
                if ok(i, s, B):
                    act.wait_ge(x_loaded[s], 96 * (i + 1))
                    if not (isinstance(i, int) and g < 2):
                        act.wait_ge(moments, g - 1)
                    stats(i, 2 * (groups_before(i, s, 0) + groups_before(i, s, 2)), xin[:, s],
                          [sums[:, s % 2, q:q + 1] for q in range(2)], sums_done)
                if ok(i, s, B):
                    act.wait_ge(var_done, g + 1)
                    act.activation(mom[:, s % 2, 3:4], mom[:, s % 2, 2:3], ACT.Ln, bias=eps[:, :]).then_inc(
                        log_done, 1)
                    act.wait_ge(log_done, g + 1)
                    act.activation(aff[:, s % 2, 0:1], mom[:, s % 2, 3:4], ACT.Exp, scale=-0.5).then_inc(
                        std_done, 1)
                if ok(i, s - 2, B):
                    act.wait_ge(x1_cleared, g - 1)
                    stats(i, 2 * (groups_before(i, s, -1) + groups_before(i, s, 2)), x1t[:, s % 2],
                          [sums1[:, q, bass.ds(g - 2, 1)] for q in range(2)], sums1_done)
            steps(act, step)
            act.wait_ge(fin_v, 2)
            act.activation(mom1[:, 3, :], mom1[:, 2, :], ACT.Ln, bias=eps[0:C, :]).then_inc(fin_a, 1)
            act.wait_ge(fin_a, 1)
            act.activation(gn2[:, 0, :], mom1[:, 3, :], ACT.Exp, scale=-0.5).then_inc(fin_a, 1)

        @block.vector
        def _(dve):
            dve.memset(eps[:, :], 1e-5).then_inc(eps_set, 1)
            dve.wait_ge(zeroed, 1)
            dve.wait_ge(w_loaded, 16)
            padded = wpd[:, BR * PITCH + BC:BR * PITCH + BC + KS * PITCH].rearrange("c (h w) -> c h w", w=PITCH)
            dve.tensor_copy(padded[:, :, 0:KS], wst[:, :].rearrange("c (h w) -> c h w", w=KS)).then_inc(w_padded, 1)
            dve.wait_ge(const_loaded, 32)

            def step(i, s):
                g = B * i + s
                for ch in range(GC):
                    k = GC * (s - 1) + ch
                    c = GC * (g - 1) + ch
                    if ch == 1 and ok(i, s, B):
                        pm = ps_tr[:, 2 + s % 2, 0:2]
                        m = mom[:, s % 2]
                        dve.wait_ge(moments, g + 1)
                        if not (isinstance(i, int) and g < 2):
                            dve.wait_ge(normed, g - 1)
                        dve.tensor_copy(m[:, 0:2], pm).then_inc(var_tmp, 1)
                        dve.wait_ge(var_tmp, 2 * g + 1)
                        dve.tensor_scalar(m[:, 2:3], m[:, 0:1], m[:, 0:1], -1.0, ALU.mult, ALU.mult).then_inc(
                            var_tmp, 1)
                        dve.wait_ge(var_tmp, 2 * g + 2)
                        dve.tensor_tensor(m[:, 2:3], m[:, 2:3], m[:, 1:2], ALU.add).then_inc(var_done, 1)
                        dve.wait_ge(std_done, g + 1)
                        dve.scalar_tensor_tensor(aff[:, s % 2, 1:2], m[:, 0:1], -1.0, aff[:, s % 2, 0:1], ALU.mult,
                                                 ALU.mult).then_inc(affine, 1)
                    if ok(i, k + 1, GC * B):
                        par = (k + 1) % 2
                        dve.wait_ge(tin_ps, c + 2)
                        if not (isinstance(i, int) and c + 1 < 2):
                            dve.wait_ge(conv_ps, c)
                        dve.tensor_copy(
                            blocks[:, par, :, BATCH:(NYB + 1) * BATCH],
                            ps_tr[:, 0:2, :].rearrange("p a (b n) -> p (a b) n", n=P)[:, 0:NXB]).then_inc(tin_done, 1)
                    if ok(i, k, GC * B):
                        gs = s - 1
                        if ch == 0 and not (isinstance(i, int) and B * i + gs < 2):
                            n2 = (B * i + gs) // 2 if isinstance(i, int) else (B // 2) * i + gs // 2
                            dve.wait_ge(x1_stored[gs % 2], 96 * n2)
                            dve.wait_ge(sums1_done, B * i + gs - 1)
                        dve.wait_ge(conv_ps, c + 1)
                        half = STRIPE // 2
                        dve.scalar_tensor_tensor(
                            x1t[:, gs % 2, ch, :].rearrange("p (a n) -> p a n", a=2),
                            ps_conv[:, 2 * (k % 2):2 * (k % 2) + 2, 0:half], biasb[:, bass.ds(c, 1)],
                            xin[:, gs % XR, ch, :].rearrange("p (a n) -> p a n", a=2), ALU.add, ALU.add).then_inc(
                                x1_done, 1)
            steps(dve, step)
            dve.wait_ge(sums1_done, GROUPS)
            for q in range(2):
                ins = dve.tensor_copy(sums1c[:, q, :].rearrange("p (g c) -> p g c", c=GC),
                                      sums1[:, q, :].unsqueeze(2).broadcast_to((P, GROUPS, GC)))
            ins.then_inc(fin_v, 1)
            dve.wait_ge(fin_p, 1)
            dve.tensor_copy(mom1[:, 0:2, :], ps_tr[0:C, 0, 0:2 * BATCH].rearrange("p (a b) -> p a b", a=2)).then_inc(
                fin_w, 1)
            dve.wait_ge(fin_w, 1)
            dve.scalar_tensor_tensor(mom1[:, 2, :], mom1[:, 0, :], -1.0, mom1[:, 0, :], ALU.mult, ALU.mult).then_inc(
                fin_w, 1)
            dve.wait_ge(fin_w, 2)
            dve.tensor_tensor(mom1[:, 2, :], mom1[:, 2, :], mom1[:, 1, :], ALU.add).then_inc(fin_v, 1)
            dve.wait_ge(fin_a, 2)
            dve.scalar_tensor_tensor(gn2[:, 1, :], mom1[:, 0, :], -1.0, gn2[:, 0, :], ALU.mult, ALU.mult).then_inc(
                fin_w, 1)
            dve.wait_ge(fin_w, 3)

        @block.tensor
        def _(pe):
            pe.wait_ge(const_loaded, 32)

            def step(i, s):
                g = B * i + s
                for ch in range(GC):
                    k = GC * (s - 1) + ch
                    c = GC * (g - 1) + ch
                    if ok(i, k + 1, GC * B):
                        ch1, gs = (ch + 1) % GC, s - 1 if ch < GC - 1 else s
                        if ch1 == 0:
                            pe.wait_ge(normed, B * i + gs + 1)
                        if not (isinstance(i, int) and c + 1 < 1):
                            pe.wait_ge(tin_done, c + 1)
                        for b in range(NXB):
                            ins = pe.transpose(ps_tr[:, b // 4, (b % 4) * P:(b % 4 + 1) * P], xn[:, gs % 2, ch1, b, :],
                                               cc("ident"))
                        ins.then_inc(tin_ps, 1)
                    if ok(i, k, GC * B):
                        par = k % 2
                        t_turn = B * i + s - 1
                        pe.wait_ge(t_loaded[ch], 16 * (t_turn + 1))
                        pe.wait_ge(tin_done, c + 1)
                        if not (isinstance(i, int) and c < 2):
                            pe.wait_ge(x1_done, c - 1)
                        for dy in (0, -1, 1):
                            for b in range(NXB):
                                x0, x1e = max(0, BC * (b - 2)), min(HW, BC * (b + 3))
                                last = dy == 1 and b == NXB - 1
                                for h in range(2):
                                    y0 = max(BR // 2 * h, 1 if dy == 1 else 0)
                                    y1 = min(BR // 2 * (h + 1), BR - 1 if dy == -1 else BR)
                                    out = ps_conv[:, 2 * par + h, 0:STRIPE // 2].rearrange("p (y x) -> p y x", x=HW)
                                    ins = pe.matmul(
                                        out[:, y0 - BR // 2 * h:y1 - BR // 2 * h, x0:x1e],
                                        blocks[:, par, b, BATCH * (1 + dy):BATCH * (1 + dy) + P],
                                        toeplitz(toep[:, ch, :], dy, b, y0, y1, x0, x1e),
                                        start=(dy == 0 and b == 0), stop=last, skip_group_check=True)
                        ins.then_inc(conv_ps, 1)
                    if ch == 0 and ok(i, s, B):
                        pe.wait_ge(sums_done, g + 1)
                        if not (isinstance(i, int) and g < 2):
                            pe.wait_ge(var_done, g - 1)
                        pe.matmul(ps_tr[:, 2 + s % 2, 0:2], cc("samebatch"), sums[:, s % 2, :],
                                  start=True, stop=True).then_inc(moments, 1)
            steps(pe, step)
            pe.wait_ge(fin_v, 1)
            for q in range(2):
                ins = pe.matmul(ps_tr[0:C, 0, q * BATCH:(q + 1) * BATCH], sums1c[:, q, :], cc("batchsum"), start=True,
                                stop=True)
            ins.then_inc(fin_p, 1)


def toeplitz(t, dy, b, y0, y1, x0, x1):
    off = PITCH * (2 * BR - 1 + BR * dy - y0) + BC * b + 3 * BC - 1 - x0
    return bass.AP(t.tensor, t.offset + off, [t.ap[0], [-PITCH, y1 - y0], [-1, x1 - x0]])


def window_pass(nc, x1, out, prm, const, gn2):
    B = NWIN
    LOAD, QKV, SMAX, SOFT, PROJ, MLPS = range(6)
    with ExitStack() as ctx:
        def sb(name, shape):
            return ctx.enter_context(nc.sbuf_tensor("b_" + name, shape, F32))

        def sem(name):
            return ctx.enter_context(nc.semaphore(name))

        cst = sb("const", [P, NCONST])
        wraw = sb("wraw", [C, 3, C])
        woraw = sb("woraw", [C, C])
        w1raw = sb("w1raw", [C, MLP])
        wqk = sb("wqk", [C, 2, P])
        wqkraw = sb("wqkraw", [C, 2, P])
        wv = sb("wv", [C, C])
        wo = sb("wo", [P, 2, 2, C])
        w1 = sb("w1s", [C, MLP])
        w2 = sb("w2s", [P, NM, C])
        cols = sb("cols", [P, 16])
        LN1S, LN1B, LN2S, LN2B, BV, BO, B2, BQ, BK, B1, EPS, BVT = 0, 1, 2, 3, 4, 5, 6, 7, 8, 9, 12, 13
        xs = sb("xs", [C, B, WIN, XW])
        t0 = sb("t0", [C, B, NT])
        gnc = sb("gnc", [C, 2])
        sq = sb("sq", [C, NT])
        lg = sb("lg", [C, NT])
        rstd = sb("rstd", [C, NT])
        h1 = sb("h1", [C, NT])
        h2 = sb("h2", [C, NT])
        q = sb("q", [P, 4, NWIN, WS])
        k = sb("k", [P, 4, NWIN, WS])
        kd = sb("kd", [P, 2, NWIN, HPG, TOK])
        qm = sb("qm", [P, NWIN, TOK])
        qd = sb("qd", [P, NWIN, HPG, TOK])
        vd = sb("vd", [P, 4, PAIRS, HEADS, 2, VA])
        mx = sb("mx", [P, PAIRS, P])
        pt = sb("pt", [P, PAIRS, HEADS * TOK + WS - TOK])
        rden = sb("rden", [P, PAIRS, HEADS // 2, 2])
        o = sb("o", [P, PAIRS, 2, WS])
        ot = sb("ot", [P, PAIRS, 2, TOK])
        t1 = sb("t1", [C, 2, NT])
        mid = sb("mid", [P, NM, NT])
        y = sb("y", [C, 2, NT])
        outs = sb("outs", [C, 2, WIN, XW])
        ps_max = ctx.enter_context(nc.psum_tensor("ps_max", [P, QG, 512], F32))
        ps_exp = ctx.enter_context(nc.psum_tensor("ps_exp", [P, QG, 512], F32))
        ps_xc = ctx.enter_context(nc.psum_tensor("ps_xc", [P, 512], F32))
        ps_var = ctx.enter_context(nc.psum_tensor("ps_var", [P, 512], F32))
        ps_ring = [ctx.enter_context(nc.psum_tensor(f"ps_ring{r}", [P, 512], F32)) for r in range(2)]

        x_loaded = [sem(f"xs_loaded{r}") for r in range(B)]
        stored = [sem(f"stored{r}") for r in range(2)]
        names = ("par_loaded zeroed_v zeroed_p wprep bias_ps bias_done gn_col wrapped t0_done xc1 sq1 var1 lg1 rstd1 "
                 "h1_done q_ps k_ps v_ps q_done k_done v_done kd_done s_ps mx_done mt_ps qm_done qd_done st_ps p_done "
                 "pv_ps rden_done o_done ot_ps ot_done wo_ps t1_done xc2 sq2 var2 lg2 rstd2 h2_done w1_ps gelu_done "
                 "w2_ps y_done added out_done").split()
        S = {n: sem("b_" + n) for n in names}

        def cc(name, rows=P):
            lo, hi = CONST[name]
            return cst[0:rows, lo:hi]

        def strip(i, s, off):
            n = B * i + s - off
            if isinstance(i, int) and not 0 <= n < BATCH * B:
                return None
            return n

        def steps(eng, step):
            for s in range(B):
                step(0, s)
            with eng.Fori(1, BATCH, 1) as i:
                for s in range(B):
                    step(i, s)
            for s in range(MLPS):
                step(BATCH, s)

        def after(eng, i, name, count):
            if not isinstance(i, int) or count > 0:
                eng.wait_ge(S[name], count)

        USES = [("ot", PROJ, "ot_done", 1, 1), ("mt", SOFT, "qm_done", 1, 1),
                ("wo", PROJ, "t1_done", 1, 1), ("w1a", MLPS, "gelu_done", 3, 1), ("w1b", MLPS, "gelu_done", 3, 2),
                ("w1c", MLPS, "gelu_done", 3, 3), ("w2", MLPS, "y_done", 1, 1), ("q", QKV, "q_done", 1, 1),
                ("k", QKV, "k_done", 1, 1), ("v", QKV, "v_done", 1, 1), ("pv", SOFT, "o_done", 1, 1)]
        NU = len(USES)

        def bank(s, use):
            u = [x[0] for x in USES].index(use)
            return ps_ring[(NU * s + u) % 2]

        def wait_bank(pe, i, s, use):
            u = NU * s + [x[0] for x in USES].index(use) - 2
            while True:
                _, off, name, per, nth = USES[u % NU]
                n = strip(i, u // NU, off)
                if n is not None:
                    pe.wait_ge(S[name], per * n + nth)
                    return
                u -= 2
                if isinstance(i, int) and B * i + u // NU < 0:
                    return

        def tokens(t):
            return t[:, :, SHIFT:SHIFT + HW].rearrange("c y (w x) -> c w y x", x=WIN)

        def windows(t):
            return t.rearrange("c (w y x) -> c w y x", y=WIN, x=WIN)

        def rows(t, img, sl):
            r0 = SHIFT + WIN * sl
            parts = [(0, r0, min(WIN, HW - r0))]
            if r0 + WIN > HW:
                parts.append((HW - r0, 0, r0 + WIN - HW))
            im = t[bass.ds(img, 1), :, :, :].rearrange("b c h w -> c (b h) w")
            return [(d, n, im[:, r:r + n, :]) for d, r, n in parts]

        def settled(pool):
            pool.nop(nofuse=True)

        NPAR = 25
        block = ctx.enter_context(nc.Block())

        @block.sync
        def _(sp):
            def load(dst, src):
                sp.dma_start(dst, src).then_inc(S["par_loaded"], 16)
                count[0] += 1
            count = [0]
            sp.wait_ge(S["zeroed_v"], 1)
            load(cst[:, :], const)
            for j, n in enumerate(("wq", "wk", "wv")):
                load(wraw[:, j, :], prm[n])
            load(woraw[:, :], prm["wo"])
            load(w1raw[:, :], prm["w1"])
            load(w2[:, :, :], prm["w2"].rearrange("(m p) n -> p m n", p=P))
            by_head = prm["wo"].rearrange("(h a d) n -> a h d n", a=2, d=DH)
            for a in range(2):
                for w in range(2):
                    for_h = wo[WS * w:WS * w + C // 2, a, w, :]
                    load(for_h, by_head[a])
            for j, n in ((LN1S, "ln1_s"), (LN1B, "ln1_b"), (LN2S, "ln2_s"), (LN2B, "ln2_b"), (BV, "bv"), (BO, "bo"),
                         (B2, "b2")):
                load(cols[0:C, j:j + 1], prm[n].rearrange("(c a) -> c a", a=1))
            for j, n in ((BQ, "bq"), (BK, "bk")):
                for g in range(QG):
                    load(cols[QR * g:QR * g + GRP, j:j + 1],
                         prm[n].rearrange("(g c a) -> g c a", g=QG, a=1)[g])
            for m in range(NM):
                load(cols[:, B1 + m:B1 + m + 1], prm["b1"].rearrange("(m p a) -> m p a", p=P, a=1)[m])
            assert count[0] == NPAR, count

            def step(i, s):
                n = strip(i, s, LOAD)
                if n is not None:
                    after(sp, i, "out_done", n - B + 1)
                    for d, cnt, src in rows(x1, i, s):
                        sp.dma_start(xs[:, s, d:d + cnt, 0:HW], src).then_inc(x_loaded[s], 16)
                n = strip(i, s, MLPS)
                if n is not None:
                    sp.wait_ge(S["out_done"], n + 1)
                    sl = (s - MLPS) % B
                    for d, cnt, dst in rows(out, i + (s - MLPS) // B, sl):
                        sp.dma_start(dst, outs[:, sl % 2, d:d + cnt, 0:HW]).then_inc(stored[sl % 2], 16)
            steps(sp, step)
            sp.wait_ge(stored[0], 16 * BATCH * 4)
            sp.wait_ge(stored[1], 16 * BATCH * 5)

        @block.gpsimd
        def _(pool):
            pool.memset(q[:, :, :, :], 0.0).then_inc(S["zeroed_p"], 1)
            pool.memset(k[:, :, :, :], 0.0).then_inc(S["zeroed_p"], 1)
            pool.memset(vd[:, :, :, :, :, :], 0.0).then_inc(S["zeroed_p"], 1)
            pool.wait_ge(S["zeroed_p"], 3)
            at = [(WS * half + lo, WS * half + hi, half) for half in range(2) for lo, hi in ((0, 32), (32, TOK))]
            for n, (lo, hi, half) in enumerate(at):
                pool.memset(vd[lo:hi, :, :, :, half, DH:VA], 1.0).then_inc(S["zeroed_p"], 1)
                pool.wait_ge(S["zeroed_p"], 4 + n)
            pool.memset(mx[:, :, :], 0.0).then_inc(S["zeroed_p"], 1)
            pool.memset(pt[:, :, :], 1.0).then_inc(S["zeroed_p"], 1)
            pool.memset(o[:, :, :, :], 0.0).then_inc(S["zeroed_p"], 1)
            pool.wait_ge(S["par_loaded"], 16 * NPAR)

            def step(i, s):
                n = strip(i, s, LOAD)
                if n is not None:
                    if s == 0:
                        after(pool, i, "t0_done", n)
                        settled(pool)
                        pool.tensor_copy(gnc[:, :].unsqueeze(2), gn2[:, :, bass.ds(i, 1)]).then_inc(S["gn_col"], 1)
                        pool.wait_ge(S["gn_col"], i + 1)
                    pool.wait_ge(x_loaded[s], (16 if s < B - 1 else 32) * (i + 1))
                    settled(pool)
                    pool.tensor_copy(xs[:, s, :, HW:XW], xs[:, s, :, 0:SHIFT]).then_inc(S["wrapped"], 1)
                    pool.wait_ge(S["wrapped"], n + 1)
                    after(pool, i, "t1_done", n - B + 1)
                    settled(pool)
                    pool.tensor_scalar(windows(t0[:, s, :]), tokens(xs[:, s]), gnc[:, 0:1], gnc[:, 1:2], ALU.mult,
                                       ALU.add).then_inc(S["t0_done"], 1)
                n = strip(i, s, SOFT)
                if n is not None:
                    pool.wait_ge(S["qm_done"], n + 1)
                    after(pool, i, "st_ps", PAIRS * n)
                    settled(pool)
                    for j in range(HPG):
                        ins = pool.tensor_scalar(qd[:, :, j, :], qm[:, :, :], cc("headmask")[:, j:j + 1], None,
                                                 ALU.mult)
                    ins.then_inc(S["qd_done"], 1)
                n = strip(i, s, MLPS)
                if n is not None:
                    sl = (s - MLPS) % B
                    pool.wait_ge(S["y_done"], n + 1)
                    img = i + (s - MLPS) // B
                    before = img * (4 if sl % 2 == 0 else 5) + sl // 2
                    if not isinstance(i, int) or before > 0:
                        pool.wait_ge(stored[sl % 2], 16 * before)
                    settled(pool)
                    pool.tensor_tensor(tokens(outs[:, sl % 2]), windows(y[:, sl % 2, :]), tokens(xs[:, sl]),
                                       ALU.add).then_inc(S["added"], 1)
                    pool.wait_ge(S["added"], n + 1)
                    settled(pool)
                    pool.tensor_copy(outs[:, sl % 2, :, 0:SHIFT], outs[:, sl % 2, :, HW:XW]).then_inc(
                        S["out_done"], 1)
                n = strip(i, s, QKV)
                if n is not None:
                    sl = (s - QKV) % B
                    pool.wait_ge(S["k_done"], n + 1)
                    after(pool, i, "s_ps", PAIRS * (n - 1))
                    settled(pool)
                    for j in range(HPG):
                        ins = pool.tensor_scalar(kd[:, sl % 2, :, j, :], k[:, sl % 4, :, 0:TOK],
                                                 cc("headmask")[:, j:j + 1], None, ALU.mult)
                    ins.then_inc(S["kd_done"], 1)
            steps(pool, step)

        @block.scalar
        def _(act):
            act.wait_ge(S["bias_done"], 3)

            def step(i, s):
                n = strip(i, s, QKV)
                if n is not None:
                    act.wait_ge(S["xc1"], n + 1)
                    after(act, i, "var2", n - (PROJ - QKV))
                    act.activation(sq[:, :], ps_xc[0:C, 0:NT], ACT.Square).then_inc(S["sq1"], 1)
                n = strip(i, s, MLPS)
                if n is not None:
                    for m, use in enumerate(("w1a", "w1b", "w1c")):
                        act.wait_ge(S["w1_ps"], NM * n + m + 1)
                        if m == 0:
                            after(act, i, "w2_ps", n)
                        act.activation(mid[:, m, :], bank(s, use)[:, 0:NT], ACT.Gelu_apprx_tanh,
                                       bias=cols[:, B1 + m:B1 + m + 1]).then_inc(S["gelu_done"], 1)
                n = strip(i, s, QKV)
                if n is not None:
                    act.wait_ge(S["var1"], n + 1)
                    act.activation(lg[:, :], ps_var[0:C, 0:NT], ACT.Ln, bias=cols[0:C, EPS:EPS + 1]).then_inc(
                        S["lg1"], 1)
                    act.wait_ge(S["lg1"], n + 1)
                    after(act, i, "h2_done", n - (PROJ - QKV))
                    act.activation(rstd[:, :], lg[:, :], ACT.Exp, scale=-0.5).then_inc(S["rstd1"], 1)
                n = strip(i, s, SOFT)
                if n is not None:
                    for p in range(PAIRS):
                        act.wait_ge(S["st_ps"], PAIRS * n + p + 1)
                        if p == 0:
                            after(act, i, "pv_ps", n)
                        act.activation(pt[:, p, 0:HEADS * TOK].rearrange("p (g n) -> p g n", g=QG),
                                       ps_exp[:, :, 0:HPG * TOK], ACT.Exp,
                                       scale=float(DH) ** -0.5).then_inc(S["p_done"], 1)
                n = strip(i, s, QKV)
                if n is not None:
                    sl = (s - QKV) % 4
                    act.wait_ge(S["k_ps"], n + 1)
                    after(act, i, "st_ps", PAIRS * (n - 3))
                    after(act, i, "kd_done", n - 3)
                    act.activation(k[:, sl, :, 0:TOK], bank(s, "k")[:, 0:NT].rearrange("p (w t) -> p w t", t=TOK),
                                   ACT.Identity, bias=cols[:, BK:BK + 1]).then_inc(S["k_done"], 1)
                n = strip(i, s, PROJ)
                if n is not None:
                    act.wait_ge(S["xc2"], n + 1)
                    n1 = strip(i, s, QKV)
                    act.wait_ge(S["var1"], n1 + 1 if n1 is not None else BATCH * B)
                    act.activation(sq[:, :], ps_xc[0:C, 0:NT], ACT.Square).then_inc(S["sq2"], 1)
                    act.wait_ge(S["var2"], n + 1)
                    act.activation(lg[:, :], ps_var[0:C, 0:NT], ACT.Ln, bias=cols[0:C, EPS:EPS + 1]).then_inc(
                        S["lg2"], 1)
                    act.wait_ge(S["lg2"], n + 1)
                    act.wait_ge(S["h1_done"], n1 + 1 if n1 is not None else BATCH * B)
                    act.activation(rstd[:, :], lg[:, :], ACT.Exp, scale=-0.5).then_inc(S["rstd2"], 1)
            steps(act, step)

        @block.vector
        def _(dve):
            dve.memset(wqkraw[:, :, :], 0.0)
            dve.memset(wo[:, :, :, :], 0.0)
            dve.memset(cols[:, :], 0.0).then_inc(S["zeroed_v"], 1)
            dve.wait_ge(S["par_loaded"], 16 * NPAR)
            dve.memset(cols[:, EPS:EPS + 1], 1e-6)
            for j in range(2):
                ins = dve.tensor_copy(wqkraw[:, j, :].rearrange("c (g r) -> c g r", r=QR)[:, :, 0:GRP],
                                      wraw[:, j, :].rearrange("c (g r) -> c g r", r=GRP))
            ins.then_inc(S["wprep"], 1)
            dve.wait_ge(S["wprep"], 1)
            for j in range(2):
                dve.tensor_scalar(wqk[:, j, :], wqkraw[:, j, :], cols[0:C, LN1S:LN1S + 1], None, ALU.mult)
            dve.tensor_scalar(wv[:, :], wraw[:, 2, :], cols[0:C, LN1S:LN1S + 1], None, ALU.mult)
            dve.tensor_scalar(w1[:, :], w1raw[:, :], cols[0:C, LN2S:LN2S + 1], None, ALU.mult).then_inc(S["wprep"], 1)
            dve.wait_ge(S["bias_ps"], 1)
            dve.tensor_tensor(cols[:, BQ:BQ + 2], cols[:, BQ:BQ + 2], ps_xc[:, 0:2], ALU.add)
            dve.tensor_tensor(cols[:, B1:B1 + NM], cols[:, B1:B1 + NM], ps_xc[:, 4:4 + NM], ALU.add)
            dve.tensor_tensor(cols[0:C, BVT:BVT + 1], cols[0:C, BV:BV + 1], ps_xc[0:C, 2:3], ALU.add).then_inc(
                S["bias_done"], 1)
            dve.wait_ge(S["bias_done"], 1)
            dve.tensor_tensor(cols[:, BK:BK + 1], cols[:, BK:BK + 1], cc("onesrows"), ALU.add).then_inc(
                S["bias_done"], 1)
            dve.wait_ge(S["bias_ps"], 2)
            dve.tensor_tensor(cols[0:C, BO:BO + 1], cols[0:C, BO:BO + 1], ps_var[0:C, 0:1], ALU.add).then_inc(
                S["bias_done"], 1)
            dve.wait_ge(S["bias_done"], 3)
            dve.wait_ge(S["zeroed_p"], 10)

            def maxima(i, n, p):
                dve.wait_ge(S["s_ps"], PAIRS * n + p + 1)
                if p == 0:
                    after(dve, i, "mt_ps", n)
                dve.tensor_reduce(mx[:, p, :].rearrange("q (g r) -> q g r", g=QG)[:, :, MAXCOL:MAXCOL + HPG],
                                  ps_max[:, :, 0:HPG * TOK].rearrange("q g (j t) -> q g j t", j=HPG),
                                  AX.X, ALU.max, negate=True).then_inc(S["mx_done"], 1)

            def step(i, s):
                n = strip(i, s, PROJ)
                if n is not None:
                    dve.wait_ge(S["ot_ps"], n + 1)
                    after(dve, i, "wo_ps", n)
                    dve.tensor_copy(ot[:, :, :, :],
                                    bank(s, "ot")[:, :].rearrange("c (p a t) -> c p a t", p=PAIRS, a=2)[:, :, :, 0:TOK]).then_inc(S["ot_done"], 1)
                n = strip(i, s, SOFT)
                if n is not None:
                    dve.wait_ge(S["mt_ps"], n + 1)
                    after(dve, i, "qd_done", n)
                    for w in range(2):
                        ins = dve.tensor_tensor(
                            qm[:, :, :].rearrange("p (a w) t -> p a w t", w=2)[:, :, w, :],
                            bank(s, "mt")[:, :].rearrange("c (p n) -> c p n", p=PAIRS)[:, :, WS * w:WS * w + TOK],
                            q[:, (s - SOFT) % 4, :, 0:TOK].rearrange("p (a w) t -> p a w t", w=2)[:, :, w, :], ALU.add)
                    ins.then_inc(S["qm_done"], 1)
                n = strip(i, s, PROJ)
                if n is not None:
                    dve.wait_ge(S["wo_ps"], n + 1)
                    after(dve, i, "y_done", n - 1)
                    after(dve, i, "xc2", n - 1)
                    dve.scalar_tensor_tensor(t1[:, (s - PROJ) % 2, :], bank(s, "wo")[0:C, 0:NT], cols[0:C, BO:BO + 1],
                                             t0[:, (s - PROJ) % B, :], ALU.add, ALU.add).then_inc(S["t1_done"], 1)
                n2 = strip(i, s, SMAX)
                if n2 is not None:
                    maxima(i, n2, 0)
                    maxima(i, n2, 1)
                n = strip(i, s, QKV)
                if n is not None:
                    dve.wait_ge(S["rstd1"], n + 1)
                    after(dve, i, "v_ps", n)
                    dve.tensor_tensor(h1[:, :], ps_xc[0:C, 0:NT], rstd[:, :], ALU.mult).then_inc(S["h1_done"], 1)
                if n2 is not None:
                    maxima(i, n2, 2)
                    maxima(i, n2, 3)
                n = strip(i, s, MLPS)
                if n is not None:
                    dve.wait_ge(S["w2_ps"], n + 1)
                    after(dve, i, "added", n - 1)
                    dve.scalar_tensor_tensor(y[:, (s - MLPS) % 2, :], bank(s, "w2")[0:C, 0:NT], cols[0:C, B2:B2 + 1],
                                             t1[:, (s - MLPS) % 2, :], ALU.add, ALU.add).then_inc(S["y_done"], 1)
                n = strip(i, s, QKV)
                if n is not None:
                    sl = (s - QKV) % 4
                    dve.wait_ge(S["q_ps"], n + 1)
                    after(dve, i, "s_ps", PAIRS * (n - 3))
                    after(dve, i, "qm_done", n - 3)
                    dve.tensor_scalar(q[:, sl, :, 0:TOK], bank(s, "q")[:, 0:NT].rearrange("p (w t) -> p w t", t=TOK),
                                      cols[:, BQ:BQ + 1], None, ALU.add).then_inc(S["q_done"], 1)
                    dve.wait_ge(S["v_ps"], n + 1)
                    after(dve, i, "pv_ps", n - 3)
                    for w in range(2):
                        r = slice(WS * w, WS * w + TOK)
                        ins = dve.tensor_copy(vd[r, sl, :, :, w, 0:DH],
                                              bank(s, "v")[r, 0:PAIRS * C].rearrange("t (p h d) -> t p h d", p=PAIRS,
                                                                                     d=DH))
                    ins.then_inc(S["v_done"], 1)
                n = strip(i, s, SOFT)
                if n is not None:
                    dve.wait_ge(S["pv_ps"], n + 1)
                    pv = bank(s, "pv")[:, 0:PAIRS * HEADS * VA].rearrange("t (p h w d) -> t p h w d", p=PAIRS,
                                                                          h=HEADS // 2, w=2)
                    pvf = bank(s, "pv")[:, 0:PAIRS * HEADS * VA].rearrange("t (p d) -> t p d", d=VA)
                    dve.reciprocal(rden[:, :, :, :].rearrange("t p h w -> t (p h w)").unsqueeze(2),
                                   pvf[:, :, DH:VA]).then_inc(S["rden_done"], 1)
                    dve.wait_ge(S["rden_done"], n + 1)
                    after(dve, i, "ot_ps", n)
                    for w in range(2):
                        ins = dve.tensor_tensor(
                            o[:, :, w, 0:C // 2].rearrange("t p (h d) -> t p h d", d=DH), pv[:, :, :, w, 0:DH],
                            rden[:, :, :, w].unsqueeze(3).broadcast_to((P, PAIRS, HEADS // 2, DH)), ALU.mult)
                    ins.then_inc(S["o_done"], 1)
                n = strip(i, s, PROJ)
                if n is not None:
                    dve.wait_ge(S["rstd2"], n + 1)
                    after(dve, i, "w1_ps", NM * n)
                    dve.tensor_tensor(h2[:, :], ps_xc[0:C, 0:NT], rstd[:, :], ALU.mult).then_inc(S["h2_done"], 1)
            steps(dve, step)

        @block.tensor
        def _(pe):
            pe.wait_ge(S["wprep"], 2)
            for j in range(2):
                pe.matmul(ps_xc[:, j:j + 1], wqkraw[:, j, :], cols[0:C, LN1B:LN1B + 1], start=True, stop=True,
                          skip_group_check=True)
            for m in range(NM):
                pe.matmul(ps_xc[:, 4 + m:5 + m], w1raw[:, m * P:(m + 1) * P], cols[0:C, LN2B:LN2B + 1], start=True,
                          stop=True, skip_group_check=True)
            pe.matmul(ps_xc[0:C, 2:3], wraw[:, 2, :], cols[0:C, LN1B:LN1B + 1], start=True, stop=True,
                      skip_group_check=True).then_inc(S["bias_ps"], 1)
            pe.wait_ge(S["bias_done"], 1)
            pe.matmul(ps_var[0:C, 0:1], woraw[:, :], cols[0:C, BVT:BVT + 1], start=True, stop=True).then_inc(
                S["bias_ps"], 1)
            pe.wait_ge(S["bias_done"], 3)
            pe.wait_ge(S["zeroed_p"], 10)

            def project(i, s, use, w, src, m, done):
                wait_bank(pe, i, s, use)
                pe.matmul(bank(s, use)[0:m, 0:NT], w, src, start=True, stop=True).then_inc(S[done], 1)

            def step(i, s):
                qkv, smax, soft, proj, mlps = (strip(i, s, x) for x in (QKV, SMAX, SOFT, PROJ, MLPS))
                if proj is not None:
                    pe.wait_ge(S["o_done"], proj + 1)
                    wait_bank(pe, i, s, "ot")
                    for p in range(PAIRS):
                        ins = pe.transpose(bank(s, "ot")[:, p * P:(p + 1) * P],
                                           o[:, p, :, :].rearrange("t w c -> t (w c)"), cc("ident"))
                    ins.then_inc(S["ot_ps"], 1)
                if qkv is not None:
                    pe.wait_ge(S["t0_done"], qkv + 1)
                    after(pe, i, "h2_done", qkv - (PROJ - QKV))
                    pe.matmul(ps_xc[0:C, 0:NT], cc("center", C), t0[:, (s - QKV) % B, :], start=True,
                              stop=True).then_inc(S["xc1"], 1)
                if soft is not None:
                    pe.wait_ge(S["mx_done"], PAIRS * (soft + 1))
                    wait_bank(pe, i, s, "mt")
                    for p in range(PAIRS):
                        ins = pe.transpose(bank(s, "mt")[:, p * P:(p + 1) * P], mx[:, p, :], cc("ident"))
                    ins.then_inc(S["mt_ps"], 1)
                if proj is not None:
                    pe.wait_ge(S["ot_done"], proj + 1)
                    wait_bank(pe, i, s, "wo")
                    dst = bank(s, "wo")[0:C, 0:NT].rearrange("c (p w t) -> c p w t", w=2, t=TOK)
                    for w in range(2):
                        for a in range(2):
                            ins = pe.matmul(dst[:, :, w, :], wo[:, a, w, :], ot[:, :, a, :], start=(a == 0),
                                            stop=(a == 1), skip_group_check=True)
                    ins.then_inc(S["wo_ps"], 1)
                if qkv is not None:
                    pe.wait_ge(S["sq1"], qkv + 1)
                    after(pe, i, "lg2", qkv - (PROJ - QKV))
                    pe.matmul(ps_var[0:C, 0:NT], cc("average", C), sq[:, :], start=True, stop=True).then_inc(
                        S["var1"], 1)
                if mlps is not None:
                    pe.wait_ge(S["h2_done"], mlps + 1)
                    for m, use in enumerate(("w1a", "w1b", "w1c")):
                        project(i, s, use, w1[:, m * P:(m + 1) * P], h2[:, :], P, "w1_ps")
                for p in range(PAIRS):
                    if smax is not None:
                        if p == 0:
                            pe.wait_ge(S["kd_done"], smax + 1)
                            pe.wait_ge(S["q_done"], smax + 1)
                        after(pe, i, "mx_done", PAIRS * smax + p)
                        pe.nop(nofuse=True)
                        for g in range(QG):
                            r = slice(QR * g, QR * g + QR)
                            for w in range(2):
                                ins = pe.matmul(ps_max[WS * w:WS * w + WS, g, 0:HPG * TOK],
                                                q[r, (s - SMAX) % 4, 2 * p + w, :],
                                                kd[r, (s - SMAX) % 2, 2 * p + w, :, :].rearrange("p j t -> p (j t)"),
                                                start=True, stop=True)
                        ins.then_inc(S["s_ps"], 1)
                    if soft is not None:
                        if p == 0:
                            pe.wait_ge(S["qd_done"], soft + 1)
                        after(pe, i, "p_done", PAIRS * soft + p)
                        pe.nop(nofuse=True)
                        for g in range(QG):
                            r = slice(QR * g, QR * g + QR)
                            for w in range(2):
                                ins = pe.matmul(ps_exp[WS * w:WS * w + WS, g, 0:HPG * TOK],
                                                k[r, (s - SOFT) % 4, 2 * p + w, :],
                                                qd[r, 2 * p + w, :, :].rearrange("p j t -> p (j t)"),
                                                start=True, stop=True)
                        ins.then_inc(S["st_ps"], 1)
                if mlps is not None:
                    wait_bank(pe, i, s, "w2")
                    for m in range(NM):
                        pe.wait_ge(S["gelu_done"], NM * mlps + m + 1)
                        ins = pe.matmul(bank(s, "w2")[0:C, 0:NT], w2[:, m, :], mid[:, m, :], start=(m == 0),
                                        stop=(m == NM - 1))
                    ins.then_inc(S["w2_ps"], 1)
                if qkv is not None:
                    pe.wait_ge(S["h1_done"], qkv + 1)
                    project(i, s, "q", wqk[:, 0, :], h1[:, :], P, "q_ps")
                    project(i, s, "k", wqk[:, 1, :], h1[:, :], P, "k_ps")
                    wait_bank(pe, i, s, "v")
                    for p in range(PAIRS):
                        for w in range(2):
                            ins = pe.matmul(bank(s, "v")[WS * w:WS * w + TOK, p * C:(p + 1) * C],
                                            h1[:, (2 * p + w) * TOK:(2 * p + w + 1) * TOK], wv[:, :], start=True,
                                            stop=True, skip_group_check=True)
                    ins.then_inc(S["v_ps"], 1)
                if proj is not None:
                    pe.wait_ge(S["t1_done"], proj + 1)
                    pe.wait_ge(S["h1_done"], qkv + 1 if qkv is not None else BATCH * B)
                    pe.matmul(ps_xc[0:C, 0:NT], cc("center", C), t1[:, (s - PROJ) % 2, :], start=True,
                              stop=True).then_inc(S["xc2"], 1)
                if soft is not None:
                    pe.wait_ge(S["v_done"], soft + 1)
                    wait_bank(pe, i, s, "pv")
                    for p in range(PAIRS):
                        pe.wait_ge(S["p_done"], PAIRS * soft + p + 1)
                        for h in range(HEADS):
                            col = (p * (HEADS // 2) + h // 2) * 2 * VA
                            ins = pe.matmul(bank(s, "pv")[WS * (h % 2):WS * (h % 2) + WS, col:col + 2 * VA],
                                            pt[:, p, h * TOK:h * TOK + WS],
                                            vd[:, (s - SOFT) % 4, p, h, :, :].rearrange("t w d -> t (w d)"),
                                            start=True, stop=True, skip_group_check=True)
                    ins.then_inc(S["pv_ps"], 1)
                if proj is not None:
                    pe.wait_ge(S["sq2"], proj + 1)
                    pe.wait_ge(S["lg1"], qkv + 1 if qkv is not None else BATCH * B)
                    pe.matmul(ps_var[0:C, 0:NT], cc("average", C), sq[:, :], start=True, stop=True).then_inc(
                        S["var2"], 1)
            steps(pe, step)


PARAMS = ("ln1_s", "ln1_b", "wq", "bq", "wk", "bk", "wv", "bv", "wo", "bo", "ln2_s", "ln2_b", "w1", "b1", "w2", "b2")


def build(nc, x, weight, conv_bias, prm, const, out):
    wpad = nc.dram_tensor("filters_padded", [C, WLEN], F32, kind="Internal").ap()
    x1 = nc.dram_tensor("x1_scratch", [BATCH, C, HW, HW], F32, kind="Internal").ap()
    with nc.sbuf_tensor("gn2", [C, 2, BATCH], F32) as gn2:
        conv_pass(nc, x, weight, conv_bias, const, wpad, x1, gn2)
        window_pass(nc, x1, out, prm, const, gn2)


def kernel(**inputs):
    import concourse.bacc as bacc
    from concourse.bass_utils import run_bass_kernel_spmd

    nc = bacc.Bacc("TRN2", target_bir_lowering=False, num_devices=1)
    arrays = {}

    def given(name, a):
        arrays[name] = np.ascontiguousarray(a)
        return nc.dram_tensor(name, arrays[name].shape, F32, kind="ExternalInput").ap()
    x = given("x", inputs["x"])
    weight = given("conv_weight", inputs["L0_conv_weight"])
    conv_bias = given("conv_bias", inputs["L0_conv_bias_term"])
    prm = {n: given(n, inputs["L1_conv_" + n]) for n in PARAMS}
    const = given("constants", constants())
    out = nc.dram_tensor("out", (BATCH, C, HW, HW), F32, kind="ExternalOutput").ap()
    build(nc, x, weight, conv_bias, prm, const, out)
    return run_bass_kernel_spmd(nc, [arrays], core_ids=[0]).results[0]["out"]
```

```python
from contextlib import ExitStack

import numpy as np
import concourse.bass as bass
from concourse import mybir

F32 = mybir.dt.float32
ALU = mybir.AluOpType
ACT = mybir.ActivationFunctionType
AX = mybir.AxisListType

P = 128
BATCH, C, HW = 32, 96, 56
NPIX = HW * HW
KS, PAD = 31, 15
GROUPS, GC = 32, 3
BR, BC = 16, 8
NYB, NXB = 4, 7
ROWS_LAST = HW - (NYB - 1) * BR
STRIPE = BR * HW
STRIPE_LAST = ROWS_LAST * HW
PITCH = KS + BC
WROWS = KS + 2 * BR
WLEN = WROWS * PITCH + 2 * BC
TLEN = (3 * BR - 1) * PITCH + 5 * BC
WIN, NWIN = 7, 8
SHIFT = 3
TOK = WIN * WIN
NT = NWIN * TOK
HEADS, DH, MLP = 12, 8, 384
QG, HPG = 2, 6
QR = P // QG
GRP = HPG * DH
NM = MLP // P
PAIRS = NWIN // 2
WS = 64
XW = HW + SHIFT
VA = DH + 1

CONST = {}
_n = 0
for _name, _w in (("ident", P), ("samebatch", P), ("batchsum", BATCH), ("headmask", HPG),
                  ("center", C), ("average", C), ("samegroup", C)):
    CONST[_name] = (_n, _n + _w)
    _n += _w
NCONST = _n


def constants():
    t = np.zeros((P, NCONST), np.float32)
    p = np.arange(P)

    def put(name, a):
        lo, hi = CONST[name]
        t[:a.shape[0], lo:hi] = a
    put("ident", np.eye(P))
    n_group = GC * NPIX
    put("samebatch", (p[:, None] % BATCH == p[None] % BATCH) / n_group)
    put("batchsum", (p[:, None] % BATCH == np.arange(BATCH)[None]) / n_group)
    r = p % QR
    put("headmask", np.stack([r // DH == j for j in range(HPG)], 1) * 1.0)
    put("center", np.eye(C) - 1.0 / C)
    put("average", np.full((C, C), 1.0 / C))
    return t


def conv_pass(nc, x, weight, conv_bias, const, wpad, x1, gn2):
    B = 4
    NIT = GROUPS // B
    XR = 4
    with ExitStack() as ctx:
        def sb(name, shape):
            return ctx.enter_context(nc.sbuf_tensor(name, shape, F32))

        def sem(name):
            return ctx.enter_context(nc.semaphore(name))

        cst = sb("a_const", [P, NCONST])
        xin = sb("xin", [P, XR, GC, STRIPE])
        xn = sb("xn", [P, 2, GC, NXB, BR * BC])
        x1t = sb("x1t", [P, 2, GC, STRIPE])
        blocks = sb("blocks", [P, 2, NXB, (NYB + 2) * BATCH])
        toep = sb("toep", [P, 3, TLEN])
        junk = sb("junk", [P, GC, STRIPE])
        sums = sb("sums", [P, 2, 2])
        mom = sb("mom", [P, 2, 4])
        aff = sb("aff", [P, 2, 2])
        sums1 = sb("sums1", [P, 2, GROUPS])
        sums1c = sb("sums1c", [P, 2, C])
        mom1 = sb("mom1", [C, 4, BATCH])
        biasb = sb("biasb", [P, C])
        eps = sb("a_eps", [P, 1])
        wst = sb("wst", [C, KS * KS])
        wpd = sb("wpd", [C, WLEN])
        ps_conv = ctx.enter_context(nc.psum_tensor("ps_conv", [P, 4, 512], F32))
        ps_tr = ctx.enter_context(nc.psum_tensor("ps_tr", [P, 4, 512], F32))

        x_loaded = [sem(f"x_loaded{r}") for r in range(XR)]
        t_loaded = [sem(f"t_loaded{r}") for r in range(3)]
        x1_stored = [sem(f"x1_stored{r}") for r in range(2)]
        const_loaded, w_loaded, w_padded, wpad_stored = (sem(n) for n in ("const_loaded", "w_loaded", "w_padded",
                                                                          "wpad_stored"))
        zeroed, eps_set, xn_zeroed = sem("zeroed"), sem("eps_set"), sem("xn_zeroed")
        var_tmp, fin_w = sem("var_tmp"), sem("fin_w")
        summed = sem("summed")
        sums_done, moments, var_done, log_done, std_done, affine = (sem(n) for n in (
            "sums_done", "moments", "var_done", "log_done", "std_done", "affine"))
        normed, tin_ps, tin_done, conv_ps, x1_done, x1_cleared, sums1_done = (sem(n) for n in (
            "normed", "tin_ps", "tin_done", "conv_ps", "x1_done", "x1_cleared",
            "sums1_done"))
        fin_v, fin_p, fin_a = sem("fin_v"), sem("fin_p"), sem("fin_a")

        def cc(name, rows=P):
            lo, hi = CONST[name]
            return cst[0:rows, lo:hi]

        def steps(eng, step):
            for s in range(B):
                step(0, s)
            with eng.Fori(1, NIT, 1) as i:
                for s in range(B):
                    step(i, s)
            for s in range(2):
                step(NIT, s)

        def ok(i, k, n):
            if isinstance(i, int):
                return 0 <= n * i + k < n * NIT
            return True

        def dram_rows(t, ch, last):
            src = t[:, bass.ds(ch, 1), :, :].rearrange("b c h w -> b (c h w)")
            if last:
                return src[:, (NYB - 1) * STRIPE:]
            return src[:, 0:(NYB - 1) * STRIPE].rearrange("b (y s) -> y b s", y=NYB - 1)

        def settled(pool):
            pool.nop(nofuse=True)

        block = ctx.enter_context(nc.Block())

        @block.sync
        def _(sp):
            sp.dma_start(cst[:, :], const).then_inc(const_loaded, 16)
            sp.dma_start(biasb[:, :], conv_bias.rearrange("(a c) -> a c", a=1).broadcast_to((P, C))).then_inc(
                const_loaded, 16)
            sp.dma_start(wst[:, :], weight.rearrange("c a h w -> c (a h w)")).then_inc(w_loaded, 16)
            sp.wait_ge(w_padded, 1)
            sp.dma_start(wpad, wpd[:, :]).then_inc(wpad_stored, 16)
            sp.wait_ge(wpad_stored, 16)

            def step(i, s):
                if ok(i, s, B):
                    if not isinstance(i, int) or i:
                        sp.wait_ge(x1_done, 3 * (B * i + s) - 3 * XR + 3)
                    for ch in range(GC):
                        c = GC * (B * i + s) + ch
                        sp.dma_start(xin[0:96, s, ch, :], dram_rows(x, c, False)).then_inc(x_loaded[s], 16)
                        sp.dma_start(xin[96:P, s, ch, 0:STRIPE_LAST], dram_rows(x, c, True)).then_inc(
                            x_loaded[s], 16)
                if ok(i, s - 1, B):
                    for ch in range(GC):
                        c = GC * (B * i + s - 1) + ch
                        if not (isinstance(i, int) and c < 3):
                            sp.wait_ge(conv_ps, c - 2)
                        src = wpad[bass.ds(c, 1), :]
                        src = bass.AP(src.tensor, src.offset, [[PITCH, BR], [1, BC], [1, TLEN]])
                        sp.dma_start(toep[:, ch, 0:TLEN], src).then_inc(t_loaded[ch], 16)
            steps(sp, step)

        @block.gpsimd
        def _(pool):
            pool.memset(wpd[:, :], 0.0).then_inc(zeroed, 1)
            for r in range(2):
                for e in (0, NYB + 1):
                    ins = pool.memset(blocks[:, r, :, e * BATCH:(e + 1) * BATCH], 0.0)
            ins.then_inc(xn_zeroed, 1)
            pool.wait_ge(xn_zeroed, 1)
            pool.memset(xin[96:P, :, :, STRIPE_LAST:], 0.0)
            pool.memset(xn[96:P, :, :, :, ROWS_LAST * BC:], 0.0).then_inc(xn_zeroed, 1)

            def step(i, s):
                if ok(i, s, B):
                    g = B * i + s
                    pool.wait_ge(affine, g + 1)
                    if not (isinstance(i, int) and g < 2):
                        pool.wait_ge(tin_ps, 3 * g - 3)
                    settled(pool)
                    for ch in range(GC):
                        for r, n in ((slice(0, 96), BR), (slice(96, P), ROWS_LAST)):
                            src = xin[r, s, ch, 0:n * HW].rearrange("p (y b c) -> p y b c", y=n, b=NXB)
                            dst = xn[r, s % 2, ch, :, 0:n * BC].rearrange("p b (y c) -> p y b c", y=n)
                            ins = pool.tensor_scalar(dst, src, aff[r, s % 2, 0:1], aff[r, s % 2, 1:2], ALU.mult,
                                                     ALU.add)
                    ins.then_inc(normed, 1)
                if ok(i, s - 2, B):
                    g = B * i + s - 2
                    pool.wait_ge(x1_done, 3 * g + 3)
                    settled(pool)
                    pool.memset(x1t[96:P, s % 2, :, STRIPE_LAST:], 0.0).then_inc(x1_cleared, 1)
                    for ch in range(GC):
                        c = GC * g + ch
                        pool.dma_start(dram_rows(x1, c, False), x1t[0:96, s % 2, ch, :]).then_inc(
                            x1_stored[s % 2], 16)
                        pool.dma_start(dram_rows(x1, c, True), x1t[96:P, s % 2, ch, 0:STRIPE_LAST]).then_inc(
                            x1_stored[s % 2], 16)
            steps(pool, step)
            for r in range(2):
                pool.wait_ge(x1_stored[r], 96 * (GROUPS // 2))

        @block.scalar
        def _(act):
            act.wait_ge(xn_zeroed, 2)
            act.wait_ge(eps_set, 1)

            def stats(i, before, src, dst, done):
                if not isinstance(i, int) or before:
                    act.wait_ge(summed, before)
                act.activation(junk[:, :, :], src, ACT.Copy, accum_out=dst[0]).then_inc(summed, 1)
                act.wait_ge(summed, before + 1)
                act.activation(junk[:, :, :], src, ACT.Square, accum_out=dst[1]).then_inc(summed, 1)
                act.wait_ge(summed, before + 2)
                act.nop().then_inc(done, 1)

            def groups_before(i, s, off):
                n = B * i + s - off
                return min(max(n, 0), GROUPS) if isinstance(i, int) else n

            def step(i, s):
                g = B * i + s
                if ok(i, s, B):
                    act.wait_ge(x_loaded[s], 96 * (i + 1))
                    if not (isinstance(i, int) and g < 2):
                        act.wait_ge(moments, g - 1)
                    stats(i, 2 * (groups_before(i, s, 0) + groups_before(i, s, 2)), xin[:, s],
                          [sums[:, s % 2, q:q + 1] for q in range(2)], sums_done)
                if ok(i, s, B):
                    act.wait_ge(var_done, g + 1)
                    act.activation(mom[:, s % 2, 3:4], mom[:, s % 2, 2:3], ACT.Ln, bias=eps[:, :]).then_inc(
                        log_done, 1)
                    act.wait_ge(log_done, g + 1)
                    act.activation(aff[:, s % 2, 0:1], mom[:, s % 2, 3:4], ACT.Exp, scale=-0.5).then_inc(
                        std_done, 1)
                if ok(i, s - 2, B):
                    act.wait_ge(x1_cleared, g - 1)
                    stats(i, 2 * (groups_before(i, s, -1) + groups_before(i, s, 2)), x1t[:, s % 2],
                          [sums1[:, q, bass.ds(g - 2, 1)] for q in range(2)], sums1_done)
            steps(act, step)
            act.wait_ge(fin_v, 2)
            act.activation(mom1[:, 3, :], mom1[:, 2, :], ACT.Ln, bias=eps[0:C, :]).then_inc(fin_a, 1)
            act.wait_ge(fin_a, 1)
            act.activation(gn2[:, 0, :], mom1[:, 3, :], ACT.Exp, scale=-0.5).then_inc(fin_a, 1)

        @block.vector
        def _(dve):
            dve.memset(eps[:, :], 1e-5).then_inc(eps_set, 1)
            dve.wait_ge(zeroed, 1)
            dve.wait_ge(w_loaded, 16)
            padded = wpd[:, BR * PITCH + BC:BR * PITCH + BC + KS * PITCH].rearrange("c (h w) -> c h w", w=PITCH)
            dve.tensor_copy(padded[:, :, 0:KS], wst[:, :].rearrange("c (h w) -> c h w", w=KS)).then_inc(w_padded, 1)
            dve.wait_ge(const_loaded, 32)

            def step(i, s):
                g = B * i + s
                for ch in range(GC):
                    k = GC * (s - 1) + ch
                    c = GC * (g - 1) + ch
                    if ch == 1 and ok(i, s, B):
                        pm = ps_tr[:, 2 + s % 2, 0:2]
                        m = mom[:, s % 2]
                        dve.wait_ge(moments, g + 1)
                        if not (isinstance(i, int) and g < 2):
                            dve.wait_ge(normed, g - 1)
                        dve.tensor_copy(m[:, 0:2], pm).then_inc(var_tmp, 1)
                        dve.wait_ge(var_tmp, 2 * g + 1)
                        dve.tensor_scalar(m[:, 2:3], m[:, 0:1], m[:, 0:1], -1.0, ALU.mult, ALU.mult).then_inc(
                            var_tmp, 1)
                        dve.wait_ge(var_tmp, 2 * g + 2)
                        dve.tensor_tensor(m[:, 2:3], m[:, 2:3], m[:, 1:2], ALU.add).then_inc(var_done, 1)
                        dve.wait_ge(std_done, g + 1)
                        dve.scalar_tensor_tensor(aff[:, s % 2, 1:2], m[:, 0:1], -1.0, aff[:, s % 2, 0:1], ALU.mult,
                                                 ALU.mult).then_inc(affine, 1)
                    if ok(i, k + 1, GC * B):
                        par = (k + 1) % 2
                        dve.wait_ge(tin_ps, c + 2)
                        if not (isinstance(i, int) and c + 1 < 2):
                            dve.wait_ge(conv_ps, c)
                        dve.tensor_copy(
                            blocks[:, par, :, BATCH:(NYB + 1) * BATCH],
                            ps_tr[:, 0:2, :].rearrange("p a (b n) -> p (a b) n", n=P)[:, 0:NXB]).then_inc(tin_done, 1)
                    if ok(i, k, GC * B):
                        gs = s - 1
                        if ch == 0 and not (isinstance(i, int) and B * i + gs < 2):
                            n2 = (B * i + gs) // 2 if isinstance(i, int) else (B // 2) * i + gs // 2
                            dve.wait_ge(x1_stored[gs % 2], 96 * n2)
                            dve.wait_ge(sums1_done, B * i + gs - 1)
                        dve.wait_ge(conv_ps, c + 1)
                        half = STRIPE // 2
                        dve.scalar_tensor_tensor(
                            x1t[:, gs % 2, ch, :].rearrange("p (a n) -> p a n", a=2),
                            ps_conv[:, 2 * (k % 2):2 * (k % 2) + 2, 0:half], biasb[:, bass.ds(c, 1)],
                            xin[:, gs % XR, ch, :].rearrange("p (a n) -> p a n", a=2), ALU.add, ALU.add).then_inc(
                                x1_done, 1)
            steps(dve, step)
            dve.wait_ge(sums1_done, GROUPS)
            for q in range(2):
                ins = dve.tensor_copy(sums1c[:, q, :].rearrange("p (g c) -> p g c", c=GC),
                                      sums1[:, q, :].unsqueeze(2).broadcast_to((P, GROUPS, GC)))
            ins.then_inc(fin_v, 1)
            dve.wait_ge(fin_p, 1)
            dve.tensor_copy(mom1[:, 0:2, :], ps_tr[0:C, 0, 0:2 * BATCH].rearrange("p (a b) -> p a b", a=2)).then_inc(
                fin_w, 1)
            dve.wait_ge(fin_w, 1)
            dve.scalar_tensor_tensor(mom1[:, 2, :], mom1[:, 0, :], -1.0, mom1[:, 0, :], ALU.mult, ALU.mult).then_inc(
                fin_w, 1)
            dve.wait_ge(fin_w, 2)
            dve.tensor_tensor(mom1[:, 2, :], mom1[:, 2, :], mom1[:, 1, :], ALU.add).then_inc(fin_v, 1)
            dve.wait_ge(fin_a, 2)
            dve.scalar_tensor_tensor(gn2[:, 1, :], mom1[:, 0, :], -1.0, gn2[:, 0, :], ALU.mult, ALU.mult).then_inc(
                fin_w, 1)
            dve.wait_ge(fin_w, 3)

        @block.tensor
        def _(pe):
            pe.wait_ge(const_loaded, 32)

            def step(i, s):
                g = B * i + s
                for ch in range(GC):
                    k = GC * (s - 1) + ch
                    c = GC * (g - 1) + ch
                    if ok(i, k + 1, GC * B):
                        ch1, gs = (ch + 1) % GC, s - 1 if ch < GC - 1 else s
                        if ch1 == 0:
                            pe.wait_ge(normed, B * i + gs + 1)
                        if not (isinstance(i, int) and c + 1 < 1):
                            pe.wait_ge(tin_done, c + 1)
                        for b in range(NXB):
                            ins = pe.transpose(ps_tr[:, b // 4, (b % 4) * P:(b % 4 + 1) * P], xn[:, gs % 2, ch1, b, :],
                                               cc("ident"))
                        ins.then_inc(tin_ps, 1)
                    if ok(i, k, GC * B):
                        par = k % 2
                        t_turn = B * i + s - 1
                        pe.wait_ge(t_loaded[ch], 16 * (t_turn + 1))
                        pe.wait_ge(tin_done, c + 1)
                        if not (isinstance(i, int) and c < 2):
                            pe.wait_ge(x1_done, c - 1)
                        for dy in (0, -1, 1):
                            for b in range(NXB):
                                x0, x1e = max(0, BC * (b - 2)), min(HW, BC * (b + 3))
                                last = dy == 1 and b == NXB - 1
                                for h in range(2):
                                    y0 = max(BR // 2 * h, 1 if dy == 1 else 0)
                                    y1 = min(BR // 2 * (h + 1), BR - 1 if dy == -1 else BR)
                                    out = ps_conv[:, 2 * par + h, 0:STRIPE // 2].rearrange("p (y x) -> p y x", x=HW)
                                    ins = pe.matmul(
                                        out[:, y0 - BR // 2 * h:y1 - BR // 2 * h, x0:x1e],
                                        blocks[:, par, b, BATCH * (1 + dy):BATCH * (1 + dy) + P],
                                        toeplitz(toep[:, ch, :], dy, b, y0, y1, x0, x1e),
                                        start=(dy == 0 and b == 0), stop=last, skip_group_check=True)
                        ins.then_inc(conv_ps, 1)
                    if ch == 0 and ok(i, s, B):
                        pe.wait_ge(sums_done, g + 1)
                        if not (isinstance(i, int) and g < 2):
                            pe.wait_ge(var_done, g - 1)
                        pe.matmul(ps_tr[:, 2 + s % 2, 0:2], cc("samebatch"), sums[:, s % 2, :],
                                  start=True, stop=True).then_inc(moments, 1)
            steps(pe, step)
            pe.wait_ge(fin_v, 1)
            for q in range(2):
                ins = pe.matmul(ps_tr[0:C, 0, q * BATCH:(q + 1) * BATCH], sums1c[:, q, :], cc("batchsum"), start=True,
                                stop=True)
            ins.then_inc(fin_p, 1)


def toeplitz(t, dy, b, y0, y1, x0, x1):
    off = PITCH * (2 * BR - 1 + BR * dy - y0) + BC * b + 3 * BC - 1 - x0
    return bass.AP(t.tensor, t.offset + off, [t.ap[0], [-PITCH, y1 - y0], [-1, x1 - x0]])


def window_pass(nc, x1, out, prm, const, gn2):
    B = NWIN
    LOAD, QKV, ATT, PROJ, MLPS = range(5)
    with ExitStack() as ctx:
        def sb(name, shape):
            return ctx.enter_context(nc.sbuf_tensor("b_" + name, shape, F32))

        def sem(name):
            return ctx.enter_context(nc.semaphore(name))

        cst = sb("const", [P, NCONST])
        wraw = sb("wraw", [C, 3, C])
        woraw = sb("woraw", [C, C])
        w1raw = sb("w1raw", [C, MLP])
        wqk = sb("wqk", [C, 2, P])
        wqkraw = sb("wqkraw", [C, 2, P])
        wv = sb("wv", [C, 2, C // 2])
        w1 = sb("w1s", [C, MLP])
        w2 = sb("w2s", [P, NM, C])
        cols = sb("cols", [P, 16])
        LN1S, LN1B, LN2S, LN2B, BV, BO, B2, BQ, BK, B1, EPS, BVT = 0, 1, 2, 3, 4, 5, 6, 7, 8, 9, 12, 13
        xs = sb("xs", [C, B, WIN, XW])
        t0 = sb("t0", [C, B, NT])
        gnc = sb("gnc", [C, 2])
        sq = sb("sq", [C, NT])
        lg = sb("lg", [C, NT])
        rstd = sb("rstd", [C, NT])
        h1 = sb("h1", [C, NT])
        h2 = sb("h2", [C, NT])
        q = sb("q", [P, 2, NWIN, WS])
        k = sb("k", [P, NWIN, TOK])
        kd = sb("kd", [P, 2, NWIN, HPG, TOK])
        vd = sb("vd", [P, 2, NWIN, HEADS // 2, 2, VA])
        mx = sb("mx", [P, 2, HEADS])
        ss = sb("ss", [P, 2, HEADS, TOK])
        probs = sb("probs", [P, 2, HEADS, WS])
        pt = sb("probs_t", [P, 2, HEADS // 2, 2, WS])
        rden = sb("rden", [P, PAIRS * HEADS])
        o = sb("o", [P, PAIRS, C])
        ot = sb("ot", [C, PAIRS, 2, TOK])
        t1 = sb("t1", [C, 2, NT])
        mid = sb("mid", [P, NM, NT])
        y = sb("y", [C, 2, NT])
        outs = sb("outs", [C, 2, WIN, XW])
        ps_s = ctx.enter_context(nc.psum_tensor("ps_s", [P, QG, 512], F32))
        ps_t = ctx.enter_context(nc.psum_tensor("ps_t", [P, 2, 512], F32))
        ps_pv = ctx.enter_context(nc.psum_tensor("ps_pv", [P, 512], F32))
        ps_xc = ctx.enter_context(nc.psum_tensor("ps_xc", [P, 512], F32))
        ps_ring = [ctx.enter_context(nc.psum_tensor(f"ps_ring{r}", [P, 512], F32)) for r in range(2)]

        x_loaded = [sem(f"xs_loaded{r}") for r in range(B)]
        stored = [sem(f"stored{r}") for r in range(2)]
        names = ("par_loaded zeroed_v zeroed_p wprep bias_ps bias_done gn_col wrapped t0_done xc1 sq1 var1 lg1 rstd1 "
                 "h1_done q_ps k_ps v_ps q_done k_done v_done kd_done s_ps mx_done sub_done exp_done t_ps pt_done "
                 "pv_ps rden_done o_done ot_ps ot_done wo_ps t1_done xc2 sq2 var2 lg2 rstd2 h2_done w1_ps gelu_done "
                 "w2_ps y_done added out_done").split()
        S = {n: sem("b_" + n) for n in names}

        def cc(name, rows=P):
            lo, hi = CONST[name]
            return cst[0:rows, lo:hi]

        def strip(i, s, off):
            n = B * i + s - off
            if isinstance(i, int) and not 0 <= n < BATCH * B:
                return None
            return n

        def steps(eng, step):
            for s in range(B):
                step(0, s)
            with eng.Fori(1, BATCH, 1) as i:
                for s in range(B):
                    step(i, s)
            for s in range(MLPS):
                step(BATCH, s)

        def after(eng, i, name, count):
            if not isinstance(i, int) or count > 0:
                eng.wait_ge(S[name], count)

        USES = [("w1a", MLPS, "gelu_done", 3, 1), ("w1b", MLPS, "gelu_done", 3, 2), ("w1c", MLPS, "gelu_done", 3, 3),
                ("var1", QKV, "lg1", 1, 1), ("ot", PROJ, "ot_done", 1, 1), ("q", QKV, "q_done", 1, 1),
                ("k", QKV, "k_done", 1, 1), ("wo", PROJ, "t1_done", 1, 1), ("v", QKV, "v_done", 1, 1),
                ("w2", MLPS, "y_done", 1, 1), ("var2", PROJ, "lg2", 1, 1)]
        NU = len(USES)

        def bank(s, use):
            u = [x[0] for x in USES].index(use)
            return ps_ring[(NU * s + u) % 2]

        def wait_bank(pe, i, s, use):
            u = NU * s + [x[0] for x in USES].index(use) - 2
            while True:
                _, off, name, per, nth = USES[u % NU]
                n = strip(i, u // NU, off)
                if n is not None:
                    pe.wait_ge(S[name], per * n + nth)
                    return
                u -= 2
                if isinstance(i, int) and B * i + u // NU < 0:
                    return

        def tokens(t):
            return t[:, :, SHIFT:SHIFT + HW].rearrange("c y (w x) -> c w y x", x=WIN)

        def windows(t):
            return t.rearrange("c (w y x) -> c w y x", y=WIN, x=WIN)

        def rows(t, img, sl):
            r0 = SHIFT + WIN * sl
            parts = [(0, r0, min(WIN, HW - r0))]
            if r0 + WIN > HW:
                parts.append((HW - r0, 0, r0 + WIN - HW))
            im = t[bass.ds(img, 1), :, :, :].rearrange("b c h w -> c (b h) w")
            return [(d, n, im[:, r:r + n, :]) for d, r, n in parts]

        def settled(pool):
            pool.nop(nofuse=True)

        NPAR = 21
        block = ctx.enter_context(nc.Block())

        @block.sync
        def _(sp):
            def load(dst, src):
                sp.dma_start(dst, src).then_inc(S["par_loaded"], 16)
                count[0] += 1
            count = [0]
            sp.wait_ge(S["zeroed_v"], 1)
            load(cst[:, :], const)
            for j, n in enumerate(("wq", "wk", "wv")):
                load(wraw[:, j, :], prm[n])
            load(woraw[:, :], prm["wo"])
            load(w1raw[:, :], prm["w1"])
            load(w2[:, :, :], prm["w2"].rearrange("(m p) n -> p m n", p=P))
            for j, n in ((LN1S, "ln1_s"), (LN1B, "ln1_b"), (LN2S, "ln2_s"), (LN2B, "ln2_b"), (BV, "bv"), (BO, "bo"),
                         (B2, "b2")):
                load(cols[0:C, j:j + 1], prm[n].rearrange("(c a) -> c a", a=1))
            for j, n in ((BQ, "bq"), (BK, "bk")):
                for g in range(QG):
                    load(cols[QR * g:QR * g + GRP, j:j + 1],
                         prm[n].rearrange("(g c a) -> g c a", g=QG, a=1)[g])
            for m in range(NM):
                load(cols[:, B1 + m:B1 + m + 1], prm["b1"].rearrange("(m p a) -> m p a", p=P, a=1)[m])
            assert count[0] == NPAR, count

            def step(i, s):
                n = strip(i, s, LOAD)
                if n is not None:
                    after(sp, i, "out_done", n - B + 1)
                    for d, cnt, src in rows(x1, i, s):
                        sp.dma_start(xs[:, s, d:d + cnt, 0:HW], src).then_inc(x_loaded[s], 16)
                n = strip(i, s, MLPS)
                if n is not None:
                    sp.wait_ge(S["out_done"], n + 1)
                    sl = (s - MLPS) % B
                    for d, cnt, dst in rows(out, i + (s - MLPS) // B, sl):
                        sp.dma_start(dst, outs[:, sl % 2, d:d + cnt, 0:HW]).then_inc(stored[sl % 2], 16)
            steps(sp, step)
            sp.wait_ge(stored[0], 16 * BATCH * 4)
            sp.wait_ge(stored[1], 16 * BATCH * 5)

        @block.gpsimd
        def _(pool):
            pool.memset(q[:, :, :, :], 0.0).then_inc(S["zeroed_p"], 1)
            pool.memset(probs[:, :, :, :], 0.0).then_inc(S["zeroed_p"], 1)
            pool.memset(vd[:, :, :, :, :, :], 0.0).then_inc(S["zeroed_p"], 1)
            pool.wait_ge(S["zeroed_p"], 3)
            at = [(WS * half + lo, WS * half + hi, half) for half in range(2) for lo, hi in ((0, 32), (32, TOK))]
            for n, (lo, hi, half) in enumerate(at):
                pool.memset(vd[lo:hi, :, :, :, half, DH:VA], 1.0).then_inc(S["zeroed_p"], 1)
                pool.wait_ge(S["zeroed_p"], 4 + n)
            pool.memset(pt[:, :, :, :, :], 1.0).then_inc(S["zeroed_p"], 1)
            pool.wait_ge(S["par_loaded"], 16 * NPAR)

            def step(i, s):
                n = strip(i, s, LOAD)
                if n is not None:
                    if s == 0:
                        after(pool, i, "t0_done", n)
                        settled(pool)
                        pool.tensor_copy(gnc[:, :].unsqueeze(2), gn2[:, :, bass.ds(i, 1)]).then_inc(S["gn_col"], 1)
                        pool.wait_ge(S["gn_col"], i + 1)
                    pool.wait_ge(x_loaded[s], (16 if s < B - 1 else 32) * (i + 1))
                    settled(pool)
                    pool.tensor_copy(xs[:, s, :, HW:XW], xs[:, s, :, 0:SHIFT]).then_inc(S["wrapped"], 1)
                    pool.wait_ge(S["wrapped"], n + 1)
                    after(pool, i, "t1_done", n - B + 1)
                    settled(pool)
                    pool.tensor_scalar(windows(t0[:, s, :]), tokens(xs[:, s]), gnc[:, 0:1], gnc[:, 1:2], ALU.mult,
                                       ALU.add).then_inc(S["t0_done"], 1)
                n = strip(i, s, MLPS)
                if n is not None:
                    sl = (s - MLPS) % B
                    pool.wait_ge(S["y_done"], n + 1)
                    img = i + (s - MLPS) // B
                    before = img * (4 if sl % 2 == 0 else 5) + sl // 2
                    if not isinstance(i, int) or before > 0:
                        pool.wait_ge(stored[sl % 2], 16 * before)
                    settled(pool)
                    pool.tensor_tensor(tokens(outs[:, sl % 2]), windows(y[:, sl % 2, :]), tokens(xs[:, sl]),
                                       ALU.add).then_inc(S["added"], 1)
                    pool.wait_ge(S["added"], n + 1)
                    settled(pool)
                    pool.tensor_copy(outs[:, sl % 2, :, 0:SHIFT], outs[:, sl % 2, :, HW:XW]).then_inc(
                        S["out_done"], 1)
            steps(pool, step)

        @block.scalar
        def _(act):
            act.wait_ge(S["bias_done"], 2)
            act.wait_ge(S["zeroed_p"], 8)
            act.preload_act_table_set("natural_log_exp_and_others")

            def inv_std(n, var, var_ready, lg_done, r_done):
                act.wait_ge(S[var_ready], n + 1)
                act.activation(lg[:, :], var[0:C, 0:NT], ACT.Ln, bias=cols[0:C, EPS:EPS + 1]).then_inc(S[lg_done], 1)
                act.wait_ge(S[lg_done], n + 1)
                return act.activation(rstd[:, :], lg[:, :], ACT.Exp, scale=-0.5).then_inc(S[r_done], 1)

            def turned(i, m, p):
                if m is None:
                    return
                act.wait_ge(S["t_ps"], PAIRS * m + p + 1)
                after(act, i, "pv_ps", PAIRS * m + p - 1)
                act.activation(pt[:, p % 2, :, :, 0:TOK],
                               ps_t[:, :, :].rearrange("k a (b w t) -> k (a b) w t", b=4, w=2)[:, 0:HEADS // 2, :, 0:TOK],
                               ACT.Copy).then_inc(S["pt_done"], 1)

            def exps(i, m, p):
                if m is None:
                    return
                act.wait_ge(S["sub_done"], PAIRS * m + p + 1)
                after(act, i, "t_ps", PAIRS * m + p - 1)
                act.activation(probs[:, p % 2, :, 0:TOK], ss[:, p % 2, :, :], ACT.Exp,
                               scale=float(DH) ** -0.5).then_inc(S["exp_done"], 1)

            def step(i, s):
                qkv, att, proj, mlps = (strip(i, s, x) for x in (QKV, ATT, PROJ, MLPS))
                if qkv is not None:
                    act.wait_ge(S["xc1"], qkv + 1)
                    after(act, i, "var2", qkv - (PROJ - QKV))
                    act.activation(sq[:, :], ps_xc[0:C, 0:NT], ACT.Square).then_inc(S["sq1"], 1)
                turned(i, proj, PAIRS - 1)
                exps(i, att, 0)
                if mlps is not None:
                    for m, use in enumerate(("w1a", "w1b", "w1c")):
                        act.wait_ge(S["w1_ps"], NM * mlps + m + 1)
                        if m == 0:
                            after(act, i, "w2_ps", mlps)
                        if m == NM - 1:
                            turned(i, att, 0)
                        act.activation(mid[:, m, :], bank(s, use)[:, 0:NT], ACT.Gelu_apprx_tanh,
                                       bias=cols[:, B1 + m:B1 + m + 1]).then_inc(S["gelu_done"], 1)
                    act.preload_act_table_set("natural_log_exp_and_others")
                if qkv is not None:
                    after(act, i, "h2_done", qkv - (PROJ - QKV))
                    inv_std(qkv, bank(s, "var1"), "var1", "lg1", "rstd1")
                if mlps is None:
                    turned(i, att, 0)
                exps(i, att, 1)
                turned(i, att, 1)
                exps(i, att, 2)
                if qkv is not None:
                    act.wait_ge(S["k_ps"], qkv + 1)
                    after(act, i, "kd_done", qkv)
                    act.activation(k[:, :, :], bank(s, "k")[:, 0:NT].rearrange("p (w t) -> p w t", t=TOK),
                                   ACT.Identity, bias=cols[:, BK:BK + 1]).then_inc(S["k_done"], 1)
                turned(i, att, 2)
                exps(i, att, 3)
                if proj is not None:
                    act.wait_ge(S["xc2"], proj + 1)
                    act.wait_ge(S["var1"], qkv + 1 if qkv is not None else BATCH * B)
                    act.activation(sq[:, :], ps_xc[0:C, 0:NT], ACT.Square).then_inc(S["sq2"], 1)
                    act.wait_ge(S["h1_done"], qkv + 1 if qkv is not None else BATCH * B)
                    inv_std(proj, bank(s, "var2"), "var2", "lg2", "rstd2")
            steps(act, step)

        @block.vector
        def _(dve):
            dve.memset(wqkraw[:, :, :], 0.0)
            dve.memset(cols[:, :], 0.0).then_inc(S["zeroed_v"], 1)
            dve.wait_ge(S["par_loaded"], 16 * NPAR)
            dve.memset(cols[:, EPS:EPS + 1], 1e-6)
            for j in range(2):
                ins = dve.tensor_copy(wqkraw[:, j, :].rearrange("c (g r) -> c g r", r=QR)[:, :, 0:GRP],
                                      wraw[:, j, :].rearrange("c (g r) -> c g r", r=GRP))
            ins.then_inc(S["wprep"], 1)
            dve.wait_ge(S["wprep"], 1)
            for j in range(2):
                dve.tensor_scalar(wqk[:, j, :], wqkraw[:, j, :], cols[0:C, LN1S:LN1S + 1], None, ALU.mult)
            for a in range(2):
                dve.tensor_scalar(wv[:, a, :].rearrange("c (h d) -> c h d", d=DH),
                                  wraw[:, 2, :].rearrange("c (h a d) -> c h a d", a=2, d=DH)[:, :, a, :],
                                  cols[0:C, LN1S:LN1S + 1], None, ALU.mult)
            dve.tensor_scalar(w1[:, :], w1raw[:, :], cols[0:C, LN2S:LN2S + 1], None, ALU.mult).then_inc(S["wprep"], 1)
            dve.wait_ge(S["bias_ps"], 1)
            dve.tensor_tensor(cols[:, BQ:BQ + 2], cols[:, BQ:BQ + 2], ps_xc[:, 0:2], ALU.add)
            dve.tensor_tensor(cols[:, B1:B1 + NM], cols[:, B1:B1 + NM], ps_xc[:, 4:4 + NM], ALU.add)
            dve.tensor_tensor(cols[0:C, BVT:BVT + 1], cols[0:C, BV:BV + 1], ps_xc[0:C, 2:3], ALU.add).then_inc(
                S["bias_done"], 1)
            dve.wait_ge(S["bias_ps"], 2)
            dve.tensor_tensor(cols[0:C, BO:BO + 1], cols[0:C, BO:BO + 1], ps_pv[0:C, 0:1], ALU.add).then_inc(
                S["bias_done"], 1)
            dve.wait_ge(S["bias_done"], 2)
            dve.wait_ge(S["zeroed_p"], 8)

            def shift_scores(i, m, p):
                if m is None:
                    return
                scores = ps_s[:, :, 0:HPG * TOK].rearrange("q g (j t) -> q g j t", j=HPG)
                dve.wait_ge(S["s_ps"], PAIRS * m + p + 1)
                dve.tensor_reduce(mx[:, p % 2, :].rearrange("q (g j) -> q g j", g=QG), scores, AX.X,
                                  ALU.max).then_inc(S["mx_done"], 1)
                dve.wait_ge(S["mx_done"], PAIRS * m + p + 1)
                after(dve, i, "exp_done", PAIRS * m + p - 1)
                dve.tensor_tensor(ss[:, p % 2, :, :].rearrange("q (g j) t -> q g j t", g=QG), scores,
                                  mx[:, p % 2, :].rearrange("q (g j) -> q g j", g=QG).unsqueeze(3).broadcast_to(
                                      (P, QG, HPG, TOK)), ALU.subtract).then_inc(S["sub_done"], 1)

            def step(i, s):
                qkv, att, proj, mlps = (strip(i, s, x) for x in (QKV, ATT, PROJ, MLPS))
                shift_scores(i, att, 0)
                if proj is not None:
                    pv = ps_pv[:, 0:PAIRS * HEADS * VA].rearrange("q (n d) -> q n d", d=VA)
                    dve.wait_ge(S["pv_ps"], PAIRS * (proj + 1))
                    dve.reciprocal(rden[:, :].unsqueeze(2), pv[:, :, DH:VA]).then_inc(S["rden_done"], 1)
                    dve.wait_ge(S["rden_done"], proj + 1)
                    after(dve, i, "ot_ps", proj)
                    dve.tensor_tensor(o[:, :, :].rearrange("q p (h d) -> q (p h) d", d=DH), pv[:, :, 0:DH],
                                      rden[:, :].unsqueeze(2).broadcast_to((P, PAIRS * HEADS, DH)),
                                      ALU.mult).then_inc(S["o_done"], 1)
                shift_scores(i, att, 1)
                if proj is not None:
                    dve.wait_ge(S["ot_ps"], proj + 1)
                    after(dve, i, "wo_ps", proj)
                    dve.tensor_copy(ot[:, :, :, :], bank(s, "ot")[0:C, :].rearrange("c (p w t) -> c p w t", p=PAIRS, w=2)[
                        :, :, :, 0:TOK]).then_inc(S["ot_done"], 1)
                if qkv is not None:
                    dve.wait_ge(S["rstd1"], qkv + 1)
                    after(dve, i, "v_ps", qkv)
                    dve.tensor_tensor(h1[:, :], ps_xc[0:C, 0:NT], rstd[:, :], ALU.mult).then_inc(S["h1_done"], 1)
                shift_scores(i, att, 2)
                if qkv is not None:
                    dve.wait_ge(S["q_ps"], qkv + 1)
                    after(dve, i, "s_ps", PAIRS * (qkv - 1))
                    dve.tensor_scalar(q[:, (s - QKV) % 2, :, 0:TOK],
                                      bank(s, "q")[:, 0:NT].rearrange("p (w t) -> p w t", t=TOK),
                                      cols[:, BQ:BQ + 1], None, ALU.add).then_inc(S["q_done"], 1)
                if proj is not None:
                    dve.wait_ge(S["wo_ps"], proj + 1)
                    after(dve, i, "y_done", proj - 1)
                    dve.scalar_tensor_tensor(t1[:, (s - PROJ) % 2, :], bank(s, "wo")[0:C, 0:NT], cols[0:C, BO:BO + 1],
                                             t0[:, (s - PROJ) % B, :], ALU.add, ALU.add).then_inc(S["t1_done"], 1)
                shift_scores(i, att, 3)
                if qkv is not None:
                    sl = (s - QKV) % 2
                    dve.wait_ge(S["k_done"], qkv + 1)
                    after(dve, i, "s_ps", PAIRS * (qkv - 1))
                    for j in range(HPG):
                        ins = dve.tensor_scalar(kd[:, sl, :, j, :], k[:, :, :], cc("headmask")[:, j:j + 1], None,
                                                ALU.mult)
                    ins.then_inc(S["kd_done"], 1)
                    dve.wait_ge(S["v_ps"], qkv + 1)
                    after(dve, i, "pv_ps", PAIRS * (qkv - 1))
                    for a in range(2):
                        r = slice(WS * a, WS * a + TOK)
                        ins = dve.tensor_copy(vd[r, sl, :, :, a, 0:DH],
                                              bank(s, "v")[r, 0:NWIN * C // 2].rearrange("t (w h d) -> t w h d", w=NWIN,
                                                                                         d=DH))
                    ins.then_inc(S["v_done"], 1)
                if mlps is not None:
                    dve.wait_ge(S["w2_ps"], mlps + 1)
                    after(dve, i, "added", mlps - 1)
                    dve.scalar_tensor_tensor(y[:, (s - MLPS) % 2, :], bank(s, "w2")[0:C, 0:NT], cols[0:C, B2:B2 + 1],
                                             t1[:, (s - MLPS) % 2, :], ALU.add, ALU.add).then_inc(S["y_done"], 1)
                if proj is not None:
                    dve.wait_ge(S["rstd2"], proj + 1)
                    after(dve, i, "w1_ps", NM * proj)
                    dve.tensor_tensor(h2[:, :], ps_xc[0:C, 0:NT], rstd[:, :], ALU.mult).then_inc(S["h2_done"], 1)
            steps(dve, step)

        @block.tensor
        def _(pe):
            pe.wait_ge(S["wprep"], 2)
            for j in range(2):
                pe.matmul(ps_xc[:, j:j + 1], wqkraw[:, j, :], cols[0:C, LN1B:LN1B + 1], start=True, stop=True,
                          skip_group_check=True)
            for m in range(NM):
                pe.matmul(ps_xc[:, 4 + m:5 + m], w1raw[:, m * P:(m + 1) * P], cols[0:C, LN2B:LN2B + 1], start=True,
                          stop=True, skip_group_check=True)
            pe.matmul(ps_xc[0:C, 2:3], wraw[:, 2, :], cols[0:C, LN1B:LN1B + 1], start=True, stop=True,
                      skip_group_check=True).then_inc(S["bias_ps"], 1)
            pe.wait_ge(S["bias_done"], 1)
            pe.matmul(ps_pv[0:C, 0:1], woraw[:, :], cols[0:C, BVT:BVT + 1], start=True, stop=True).then_inc(
                S["bias_ps"], 1)
            pe.wait_ge(S["bias_done"], 2)
            pe.wait_ge(S["zeroed_p"], 8)

            def product(i, s, use, w, src, rows, done):
                wait_bank(pe, i, s, use)
                pe.matmul(bank(s, use)[0:rows, 0:NT], w, src, start=True, stop=True).then_inc(S[done], 1)

            def scores(i, s, m, p):
                if m is None:
                    return
                if p == 0:
                    for name in ("q_done", "kd_done"):
                        pe.wait_ge(S[name], m + 1)
                after(pe, i, "sub_done", PAIRS * m + p)
                pe.nop(nofuse=True)
                for g in range(QG):
                    r = slice(QR * g, QR * g + QR)
                    for w in range(2):
                        ins = pe.matmul(ps_s[WS * w:WS * w + WS, g, 0:HPG * TOK], q[r, (s - ATT) % 2, 2 * p + w, :],
                                        kd[r, (s - ATT) % 2, 2 * p + w, :, :].rearrange("p j t -> p (j t)"),
                                        start=True, stop=True)
                ins.then_inc(S["s_ps"], 1)

            def turn(i, m, p):
                if m is None:
                    return
                pe.wait_ge(S["exp_done"], PAIRS * m + p + 1)
                after(pe, i, "pt_done", PAIRS * m + p)
                for h in range(HEADS // 2):
                    ins = pe.transpose(ps_t[:, h // 4, (h % 4) * P:(h % 4 + 1) * P],
                                       probs[:, p % 2, 2 * h:2 * h + 2, :].rearrange("q h t -> q (h t)"), cc("ident"))
                ins.then_inc(S["t_ps"], 1)

            def times_v(i, par, m, p):
                if m is None:
                    return
                if p == 0:
                    pe.wait_ge(S["v_done"], m + 1)
                    after(pe, i, "o_done", m)
                pe.wait_ge(S["pt_done"], PAIRS * m + p + 1)
                for h in range(HEADS // 2):
                    for w in range(2):
                        col = (p * HEADS + 2 * h) * VA
                        ins = pe.matmul(ps_pv[WS * w:WS * w + WS, col:col + 2 * VA], pt[:, p % 2, h, w, :],
                                        vd[:, par, 2 * p + w, h, :, :].rearrange("k a d -> k (a d)"), start=True,
                                        stop=True, skip_group_check=True)
                ins.then_inc(S["pv_ps"], 1)

            def step(i, s):
                qkv, att, proj, mlps = (strip(i, s, x) for x in (QKV, ATT, PROJ, MLPS))
                scores(i, s, att, 0)
                turn(i, proj, PAIRS - 1)
                if qkv is not None:
                    pe.wait_ge(S["t0_done"], qkv + 1)
                    after(pe, i, "h2_done", qkv - (PROJ - QKV))
                    pe.matmul(ps_xc[0:C, 0:NT], cc("center", C), t0[:, (s - QKV) % B, :], start=True,
                              stop=True).then_inc(S["xc1"], 1)
                if mlps is not None:
                    pe.wait_ge(S["h2_done"], mlps + 1)
                    product(i, s, "w1a", w1[:, 0:P], h2[:, :], P, "w1_ps")
                    product(i, s, "w1b", w1[:, P:2 * P], h2[:, :], P, "w1_ps")
                times_v(i, (s - PROJ) % 2, proj, PAIRS - 1)

                scores(i, s, att, 1)
                turn(i, att, 0)
                if mlps is not None:
                    product(i, s, "w1c", w1[:, 2 * P:3 * P], h2[:, :], P, "w1_ps")
                if qkv is not None:
                    pe.wait_ge(S["sq1"], qkv + 1)
                    product(i, s, "var1", cc("average", C), sq[:, :], C, "var1")
                if proj is not None:
                    pe.wait_ge(S["o_done"], proj + 1)
                    wait_bank(pe, i, s, "ot")
                    for p in range(PAIRS):
                        ins = pe.transpose(bank(s, "ot")[0:C, p * P:(p + 1) * P], o[:, p, :], cc("ident"))
                    ins.then_inc(S["ot_ps"], 1)
                times_v(i, (s - ATT) % 2, att, 0)

                scores(i, s, att, 2)
                turn(i, att, 1)
                if qkv is not None:
                    pe.wait_ge(S["h1_done"], qkv + 1)
                    product(i, s, "q", wqk[:, 0, :], h1[:, :], P, "q_ps")
                    product(i, s, "k", wqk[:, 1, :], h1[:, :], P, "k_ps")
                if proj is not None:
                    pe.wait_ge(S["ot_done"], proj + 1)
                    product(i, s, "wo", woraw[:, :], ot[:, :, :, :].rearrange("c p w t -> c (p w t)"), C, "wo_ps")
                times_v(i, (s - ATT) % 2, att, 1)

                scores(i, s, att, 3)
                turn(i, att, 2)
                if qkv is not None:
                    wait_bank(pe, i, s, "v")
                    for w in range(NWIN):
                        for a in range(2):
                            ins = pe.matmul(bank(s, "v")[WS * a:WS * a + TOK, w * C // 2:(w + 1) * C // 2],
                                            h1[:, w * TOK:(w + 1) * TOK], wv[:, a, :], start=True, stop=True,
                                            skip_group_check=True)
                    ins.then_inc(S["v_ps"], 1)
                if proj is not None:
                    pe.wait_ge(S["t1_done"], proj + 1)
                    pe.wait_ge(S["h1_done"], qkv + 1 if qkv is not None else BATCH * B)
                    pe.matmul(ps_xc[0:C, 0:NT], cc("center", C), t1[:, (s - PROJ) % 2, :], start=True,
                              stop=True).then_inc(S["xc2"], 1)
                if mlps is not None:
                    wait_bank(pe, i, s, "w2")
                    for m in range(NM):
                        pe.wait_ge(S["gelu_done"], NM * mlps + m + 1)
                        ins = pe.matmul(bank(s, "w2")[0:C, 0:NT], w2[:, m, :], mid[:, m, :], start=(m == 0),
                                        stop=(m == NM - 1))
                    ins.then_inc(S["w2_ps"], 1)
                times_v(i, (s - ATT) % 2, att, 2)
                if proj is not None:
                    pe.wait_ge(S["sq2"], proj + 1)
                    product(i, s, "var2", cc("average", C), sq[:, :], C, "var2")
            steps(pe, step)


PARAMS = ("ln1_s", "ln1_b", "wq", "bq", "wk", "bk", "wv", "bv", "wo", "bo", "ln2_s", "ln2_b", "w1", "b1", "w2", "b2")


def build(nc, x, weight, conv_bias, prm, const, out):
    wpad = nc.dram_tensor("filters_padded", [C, WLEN], F32, kind="Internal").ap()
    x1 = nc.dram_tensor("x1_scratch", [BATCH, C, HW, HW], F32, kind="Internal").ap()
    with nc.sbuf_tensor("gn2", [C, 2, BATCH], F32) as gn2:
        conv_pass(nc, x, weight, conv_bias, const, wpad, x1, gn2)
        window_pass(nc, x1, out, prm, const, gn2)


def kernel(**inputs):
    import concourse.bacc as bacc
    from concourse.bass_utils import run_bass_kernel_spmd

    nc = bacc.Bacc("TRN2", target_bir_lowering=False, num_devices=1)
    arrays = {}

    def given(name, a):
        arrays[name] = np.ascontiguousarray(a)
        return nc.dram_tensor(name, arrays[name].shape, F32, kind="ExternalInput").ap()
    x = given("x", inputs["x"])
    weight = given("conv_weight", inputs["L0_conv_weight"])
    conv_bias = given("conv_bias", inputs["L0_conv_bias_term"])
    prm = {n: given(n, inputs["L1_conv_" + n]) for n in PARAMS}
    const = given("constants", constants())
    out = nc.dram_tensor("out", (BATCH, C, HW, HW), F32, kind="ExternalOutput").ap()
    build(nc, x, weight, conv_bias, prm, const, out)
    return run_bass_kernel_spmd(nc, [arrays], core_ids=[0]).results[0]["out"]
```

```python
from contextlib import ExitStack

import numpy as np
import concourse.bass as bass
from concourse import mybir

F32 = mybir.dt.float32
F32R = mybir.dt.float32r
ALU = mybir.AluOpType
ACT = mybir.ActivationFunctionType
AX = mybir.AxisListType

P = 128
BATCH, C, HW = 32, 96, 56
NPIX = HW * HW
KS, PAD = 31, 15
GROUPS, GC = 32, 3
BR, BC = 16, 8
NYB, NXB = 4, 7
ROWS_LAST = HW - (NYB - 1) * BR
STRIPE = BR * HW
STRIPE_LAST = ROWS_LAST * HW
PITCH = KS + BC
WROWS = KS + 2 * BR
WLEN = WROWS * PITCH + 2 * BC
TLEN = (3 * BR - 1) * PITCH + 5 * BC
WIN, NWIN = 7, 8
SHIFT = 3
TOK = WIN * WIN
NT = NWIN * TOK
HEADS, DH, MLP = 12, 8, 384
QG, HPG = 2, 6
QR = P // QG
GRP = HPG * DH
NM = MLP // P
PAIRS = NWIN // 2
WS = 64
XW = HW + SHIFT
VA = DH + 1

CONST = {}
_n = 0
for _name, _w in (("ident", P), ("samebatch", P), ("batchsum", BATCH), ("headmask", HPG),
                  ("center", C), ("average", C), ("centre_c", C)):
    CONST[_name] = (_n, _n + _w)
    _n += _w
NCONST = _n


def constants():
    t = np.zeros((P, NCONST), np.float32)
    p = np.arange(P)

    def put(name, a):
        lo, hi = CONST[name]
        t[:a.shape[0], lo:hi] = a
    put("ident", np.eye(P))
    n_group = GC * NPIX
    put("samebatch", (p[:, None] % BATCH == p[None] % BATCH) / n_group)
    put("batchsum", (p[:, None] % BATCH == np.arange(BATCH)[None]) / n_group)
    r = p % QR
    put("headmask", np.stack([r // DH == j for j in range(HPG)], 1) * 1.0)
    put("center", np.eye(C) - 1.0 / C)
    put("average", np.full((C, C), 1.0 / C))
    put("centre_c", C * np.eye(C) - 1)
    return t


def conv_pass(nc, x, weight, conv_bias, const, wpad, x1, gn2):
    B = 4
    NIT = GROUPS // B
    XR = 4
    with ExitStack() as ctx:
        def sb(name, shape, dtype=F32):
            return ctx.enter_context(nc.sbuf_tensor(name, shape, dtype))

        def sem(name):
            return ctx.enter_context(nc.semaphore(name))

        cst = sb("a_const", [P, NCONST])
        xin = sb("xin", [P, XR, GC, STRIPE])
        xn = sb("xn", [P, 2, GC, NXB, BR * BC])
        x1t = sb("x1t", [P, 2, GC, STRIPE])
        blocks_hi = sb("blocks_hi", [P, 2, NXB, (NYB + 2) * BATCH], F32R)
        blocks_lo = sb("blocks_lo", [P, 2, NXB, (NYB + 2) * BATCH], F32R)
        toep = sb("toep", [P, 3, TLEN])
        toep_hi = sb("toep_hi", [P, 2, TLEN], F32R)
        toep_lo = sb("toep_lo", [P, 2, TLEN], F32R)
        junk = sb("junk", [P, GC, STRIPE])
        sums = sb("sums", [P, 2, 2])
        mom = sb("mom", [P, 2, 4])
        aff = sb("aff", [P, 2, 2])
        sums1 = sb("sums1", [P, 2, GROUPS])
        sums1c = sb("sums1c", [P, 2, C])
        mom1 = sb("mom1", [C, 4, BATCH])
        biasb = sb("biasb", [P, C])
        eps = sb("a_eps", [P, 1])
        wst = sb("wst", [C, KS * KS])
        wpd = sb("wpd", [C, WLEN])
        ps_conv = ctx.enter_context(nc.psum_tensor("ps_conv", [P, 4, 512], F32))
        ps_tr = ctx.enter_context(nc.psum_tensor("ps_tr", [P, 4, 512], F32))

        x_loaded = [sem(f"x_loaded{r}") for r in range(XR)]
        t_loaded = [sem(f"t_loaded{r}") for r in range(3)]
        x1_stored = [sem(f"x1_stored{r}") for r in range(2)]
        const_loaded, w_loaded, w_padded, wpad_stored = (sem(n) for n in ("const_loaded", "w_loaded", "w_padded",
                                                                          "wpad_stored"))
        zeroed, eps_set, xn_zeroed = sem("zeroed"), sem("eps_set"), sem("xn_zeroed")
        var_tmp, fin_w = sem("var_tmp"), sem("fin_w")
        summed, t_high, t_split, tin_high = (sem(n) for n in ("summed", "t_high", "t_split", "tin_high"))
        sums_done, moments, var_done, log_done, std_done, affine = (sem(n) for n in (
            "sums_done", "moments", "var_done", "log_done", "std_done", "affine"))
        normed, tin_ps, tin_done, conv_ps, x1_done, x1_cleared, sums1_done = (sem(n) for n in (
            "normed", "tin_ps", "tin_done", "conv_ps", "x1_done", "x1_cleared",
            "sums1_done"))
        fin_v, fin_p, fin_a = sem("fin_v"), sem("fin_p"), sem("fin_a")

        def cc(name, rows=P):
            lo, hi = CONST[name]
            return cst[0:rows, lo:hi]

        def steps(eng, step):
            for s in range(B):
                step(0, s)
            with eng.Fori(1, NIT, 1) as i:
                for s in range(B):
                    step(i, s)
            for s in range(2):
                step(NIT, s)

        def ok(i, k, n):
            if isinstance(i, int):
                return 0 <= n * i + k < n * NIT
            return True

        def dram_rows(t, ch, last):
            src = t[:, bass.ds(ch, 1), :, :].rearrange("b c h w -> b (c h w)")
            if last:
                return src[:, (NYB - 1) * STRIPE:]
            return src[:, 0:(NYB - 1) * STRIPE].rearrange("b (y s) -> y b s", y=NYB - 1)

        def settled(pool):
            pool.nop(nofuse=True)

        block = ctx.enter_context(nc.Block())

        @block.sync
        def _(sp):
            sp.dma_start(cst[:, :], const).then_inc(const_loaded, 16)
            sp.dma_start(biasb[:, :], conv_bias.rearrange("(a c) -> a c", a=1).broadcast_to((P, C))).then_inc(
                const_loaded, 16)
            sp.dma_start(wst[:, :], weight.rearrange("c a h w -> c (a h w)")).then_inc(w_loaded, 16)
            sp.wait_ge(w_padded, 1)
            sp.dma_start(wpad, wpd[:, :]).then_inc(wpad_stored, 16)
            sp.wait_ge(wpad_stored, 16)

            def step(i, s):
                if ok(i, s, B):
                    if not isinstance(i, int) or i:
                        sp.wait_ge(x1_done, 3 * (B * i + s) - 3 * XR + 3)
                    for ch in range(GC):
                        c = GC * (B * i + s) + ch
                        sp.dma_start(xin[0:96, s, ch, :], dram_rows(x, c, False)).then_inc(x_loaded[s], 16)
                        sp.dma_start(xin[96:P, s, ch, 0:STRIPE_LAST], dram_rows(x, c, True)).then_inc(
                            x_loaded[s], 16)
                if ok(i, s - 1, B):
                    for ch in range(GC):
                        c = GC * (B * i + s - 1) + ch
                        if not (isinstance(i, int) and c < 3):
                            sp.wait_ge(t_split, c - 2)
                        src = wpad[bass.ds(c, 1), :]
                        src = bass.AP(src.tensor, src.offset, [[PITCH, BR], [1, BC], [1, TLEN]])
                        sp.dma_start(toep[:, ch, 0:TLEN], src).then_inc(t_loaded[ch], 16)
            steps(sp, step)

        @block.gpsimd
        def _(pool):
            pool.memset(wpd[:, :], 0.0).then_inc(zeroed, 1)
            for t in (blocks_hi, blocks_lo):
                for r in range(2):
                    for e in (0, NYB + 1):
                        ins = pool.memset(t[:, r, :, e * BATCH:(e + 1) * BATCH].bitcast(F32), 0.0)
            ins.then_inc(xn_zeroed, 1)
            pool.wait_ge(xn_zeroed, 1)
            pool.memset(xin[96:P, :, :, STRIPE_LAST:], 0.0)
            pool.memset(xn[96:P, :, :, :, ROWS_LAST * BC:], 0.0).then_inc(xn_zeroed, 1)

            def step(i, s):
                if ok(i, s, B):
                    g = B * i + s
                    pool.wait_ge(affine, g + 1)
                    if not (isinstance(i, int) and g < 2):
                        pool.wait_ge(tin_ps, 3 * g - 3)
                    settled(pool)
                    for ch in range(GC):
                        for r, n in ((slice(0, 96), BR), (slice(96, P), ROWS_LAST)):
                            src = xin[r, s, ch, 0:n * HW].rearrange("p (y b c) -> p y b c", y=n, b=NXB)
                            dst = xn[r, s % 2, ch, :, 0:n * BC].rearrange("p b (y c) -> p y b c", y=n)
                            ins = pool.tensor_scalar(dst, src, aff[r, s % 2, 0:1], aff[r, s % 2, 1:2], ALU.mult,
                                                     ALU.add)
                    ins.then_inc(normed, 1)
                if ok(i, s - 2, B):
                    g = B * i + s - 2
                    pool.wait_ge(x1_done, 3 * g + 3)
                    settled(pool)
                    pool.memset(x1t[96:P, s % 2, :, STRIPE_LAST:], 0.0).then_inc(x1_cleared, 1)
                    for ch in range(GC):
                        c = GC * g + ch
                        pool.dma_start(dram_rows(x1, c, False), x1t[0:96, s % 2, ch, :]).then_inc(
                            x1_stored[s % 2], 16)
                        pool.dma_start(dram_rows(x1, c, True), x1t[96:P, s % 2, ch, 0:STRIPE_LAST]).then_inc(
                            x1_stored[s % 2], 16)
            steps(pool, step)
            for r in range(2):
                pool.wait_ge(x1_stored[r], 96 * (GROUPS // 2))

        @block.scalar
        def _(act):
            act.wait_ge(xn_zeroed, 2)
            act.wait_ge(eps_set, 1)

            def stats(i, before, src, dst, done):
                if not isinstance(i, int) or before:
                    act.wait_ge(summed, before)
                act.activation(junk[:, :, :], src, ACT.Copy, accum_out=dst[0]).then_inc(summed, 1)
                act.wait_ge(summed, before + 1)
                act.activation(junk[:, :, :], src, ACT.Square, accum_out=dst[1]).then_inc(summed, 1)
                act.wait_ge(summed, before + 2)
                act.nop().then_inc(done, 1)

            def groups_before(i, s, off):
                n = B * i + s - off
                return min(max(n, 0), GROUPS) if isinstance(i, int) else n

            def step(i, s):
                g = B * i + s
                if ok(i, s, B):
                    act.wait_ge(x_loaded[s], 96 * (i + 1))
                    if not (isinstance(i, int) and g < 2):
                        act.wait_ge(moments, g - 1)
                    stats(i, 2 * (groups_before(i, s, 0) + groups_before(i, s, 2)), xin[:, s],
                          [sums[:, s % 2, q:q + 1] for q in range(2)], sums_done)
                for ch in range(GC):
                    k = GC * (s - 1) + ch
                    c = GC * (g - 1) + ch
                    if ch == 1 and ok(i, s, B):
                        act.wait_ge(var_done, g + 1)
                        act.activation(mom[:, s % 2, 3:4], mom[:, s % 2, 2:3], ACT.Ln, bias=eps[:, :]).then_inc(
                            log_done, 1)
                        act.wait_ge(log_done, g + 1)
                        act.activation(aff[:, s % 2, 0:1], mom[:, s % 2, 3:4], ACT.Exp, scale=-0.5).then_inc(
                            std_done, 1)
                    if ok(i, k + 1, GC * B):
                        act.wait_ge(t_loaded[(ch + 1) % GC], 16 * (g if ch < GC - 1 else g + 1))
                        if not (isinstance(i, int) and c + 1 < 2):
                            act.wait_ge(conv_ps, c)
                        act.activation(toep_hi[:, (k + 1) % 2, :], toep[:, (ch + 1) % GC, :], ACT.Copy).then_inc(
                            t_high, 1)
                        act.wait_ge(tin_ps, c + 2)
                        act.activation(blocks_hi[:, (k + 1) % 2, :, BATCH:(NYB + 1) * BATCH],
                                       ps_tr[:, 0:2, :].rearrange("p a (b n) -> p (a b) n", n=P)[:, 0:NXB],
                                       ACT.Copy).then_inc(tin_high, 1)
                if ok(i, s - 2, B):
                    act.wait_ge(x1_cleared, g - 1)
                    stats(i, 2 * (groups_before(i, s, -1) + groups_before(i, s, 2)), x1t[:, s % 2],
                          [sums1[:, q, bass.ds(g - 2, 1)] for q in range(2)], sums1_done)
            steps(act, step)
            act.wait_ge(fin_v, 2)
            act.activation(mom1[:, 3, :], mom1[:, 2, :], ACT.Ln, bias=eps[0:C, :]).then_inc(fin_a, 1)
            act.wait_ge(fin_a, 1)
            act.activation(gn2[:, 0, :], mom1[:, 3, :], ACT.Exp, scale=-0.5).then_inc(fin_a, 1)

        @block.vector
        def _(dve):
            dve.memset(eps[:, :], 1e-5).then_inc(eps_set, 1)
            dve.wait_ge(zeroed, 1)
            dve.wait_ge(w_loaded, 16)
            padded = wpd[:, BR * PITCH + BC:BR * PITCH + BC + KS * PITCH].rearrange("c (h w) -> c h w", w=PITCH)
            dve.tensor_copy(padded[:, :, 0:KS], wst[:, :].rearrange("c (h w) -> c h w", w=KS)).then_inc(w_padded, 1)
            dve.wait_ge(const_loaded, 32)

            def step(i, s):
                g = B * i + s
                for ch in range(GC):
                    k = GC * (s - 1) + ch
                    c = GC * (g - 1) + ch
                    if ch == 1 and ok(i, s, B):
                        pm = ps_tr[:, 2 + s % 2, 0:2]
                        m = mom[:, s % 2]
                        dve.wait_ge(moments, g + 1)
                        if not (isinstance(i, int) and g < 2):
                            dve.wait_ge(normed, g - 1)
                        dve.tensor_copy(m[:, 0:2], pm).then_inc(var_tmp, 1)
                        dve.wait_ge(var_tmp, 2 * g + 1)
                        dve.tensor_scalar(m[:, 2:3], m[:, 0:1], m[:, 0:1], -1.0, ALU.mult, ALU.mult).then_inc(
                            var_tmp, 1)
                        dve.wait_ge(var_tmp, 2 * g + 2)
                        dve.tensor_tensor(m[:, 2:3], m[:, 2:3], m[:, 1:2], ALU.add).then_inc(var_done, 1)
                        dve.wait_ge(std_done, g + 1)
                        dve.scalar_tensor_tensor(aff[:, s % 2, 1:2], m[:, 0:1], -1.0, aff[:, s % 2, 0:1], ALU.mult,
                                                 ALU.mult).then_inc(affine, 1)
                    if ok(i, k + 1, GC * B):
                        par = (k + 1) % 2
                        dve.wait_ge(t_high, c + 2)
                        dve.tensor_tensor(toep_lo[:, par, :], toep[:, (ch + 1) % GC, :], toep_hi[:, par, :],
                                          ALU.subtract).then_inc(t_split, 1)
                        dve.wait_ge(tin_high, c + 2)
                        dve.tensor_tensor(
                            blocks_lo[:, par, :, BATCH:(NYB + 1) * BATCH],
                            ps_tr[:, 0:2, :].rearrange("p a (b n) -> p (a b) n", n=P)[:, 0:NXB],
                            blocks_hi[:, par, :, BATCH:(NYB + 1) * BATCH], ALU.subtract).then_inc(tin_done, 1)
                    if ok(i, k, GC * B):
                        gs = s - 1
                        if ch == 0 and not (isinstance(i, int) and B * i + gs < 2):
                            n2 = (B * i + gs) // 2 if isinstance(i, int) else (B // 2) * i + gs // 2
                            dve.wait_ge(x1_stored[gs % 2], 96 * n2)
                            dve.wait_ge(sums1_done, B * i + gs - 1)
                        dve.wait_ge(conv_ps, c + 1)
                        half = STRIPE // 2
                        dve.scalar_tensor_tensor(
                            x1t[:, gs % 2, ch, :].rearrange("p (a n) -> p a n", a=2),
                            ps_conv[:, 2 * (k % 2):2 * (k % 2) + 2, 0:half], biasb[:, bass.ds(c, 1)],
                            xin[:, gs % XR, ch, :].rearrange("p (a n) -> p a n", a=2), ALU.add, ALU.add).then_inc(
                                x1_done, 1)
            steps(dve, step)
            dve.wait_ge(sums1_done, GROUPS)
            for q in range(2):
                ins = dve.tensor_copy(sums1c[:, q, :].rearrange("p (g c) -> p g c", c=GC),
                                      sums1[:, q, :].unsqueeze(2).broadcast_to((P, GROUPS, GC)))
            ins.then_inc(fin_v, 1)
            dve.wait_ge(fin_p, 1)
            dve.tensor_copy(mom1[:, 0:2, :], ps_tr[0:C, 0, 0:2 * BATCH].rearrange("p (a b) -> p a b", a=2)).then_inc(
                fin_w, 1)
            dve.wait_ge(fin_w, 1)
            dve.scalar_tensor_tensor(mom1[:, 2, :], mom1[:, 0, :], -1.0, mom1[:, 0, :], ALU.mult, ALU.mult).then_inc(
                fin_w, 1)
            dve.wait_ge(fin_w, 2)
            dve.tensor_tensor(mom1[:, 2, :], mom1[:, 2, :], mom1[:, 1, :], ALU.add).then_inc(fin_v, 1)
            dve.wait_ge(fin_a, 2)
            dve.scalar_tensor_tensor(gn2[:, 1, :], mom1[:, 0, :], -1.0, gn2[:, 0, :], ALU.mult, ALU.mult).then_inc(
                fin_w, 1)
            dve.wait_ge(fin_w, 3)

        @block.tensor
        def _(pe):
            pe.wait_ge(const_loaded, 32)

            def step(i, s):
                g = B * i + s
                for ch in range(GC):
                    k = GC * (s - 1) + ch
                    c = GC * (g - 1) + ch
                    if ok(i, k + 1, GC * B):
                        ch1, gs = (ch + 1) % GC, s - 1 if ch < GC - 1 else s
                        if ch1 == 0:
                            pe.wait_ge(normed, B * i + gs + 1)
                        if not (isinstance(i, int) and c + 1 < 1):
                            pe.wait_ge(tin_done, c + 1)
                        for b in range(NXB):
                            ins = pe.transpose(ps_tr[:, b // 4, (b % 4) * P:(b % 4 + 1) * P], xn[:, gs % 2, ch1, b, :],
                                               cc("ident"))
                        ins.then_inc(tin_ps, 1)
                    if ok(i, k, GC * B):
                        par = k % 2
                        pe.wait_ge(t_split, c + 1)
                        pe.wait_ge(tin_done, c + 1)
                        if not (isinstance(i, int) and c < 2):
                            pe.wait_ge(x1_done, c - 1)
                        for dy in (0, -1, 1):
                            for b in range(NXB):
                                x0, x1e = max(0, BC * (b - 2)), min(HW, BC * (b + 3))
                                last = dy == 1 and b == NXB - 1
                                pixels = slice(BATCH * (1 + dy), BATCH * (1 + dy) + P)
                                for data, taps in ((blocks_hi, toep_hi), (blocks_hi, toep_lo), (blocks_lo, toep_hi)):
                                    for h in range(2):
                                        y0 = max(BR // 2 * h, 1 if dy == 1 else 0)
                                        y1 = min(BR // 2 * (h + 1), BR - 1 if dy == -1 else BR)
                                        out = ps_conv[:, 2 * par + h, 0:STRIPE // 2].rearrange("p (y x) -> p y x",
                                                                                              x=HW)
                                        ins = pe.matmul(
                                            out[:, y0 - BR // 2 * h:y1 - BR // 2 * h, x0:x1e],
                                            data[:, par, b, pixels],
                                            toeplitz(taps[:, par, :], dy, b, y0, y1, x0, x1e),
                                            start=(dy == 0 and b == 0 and data is blocks_hi and taps is toep_hi),
                                            stop=last, skip_group_check=True)
                        ins.then_inc(conv_ps, 1)
                    if ch == 0 and ok(i, s, B):
                        pe.wait_ge(sums_done, g + 1)
                        if not (isinstance(i, int) and g < 2):
                            pe.wait_ge(var_done, g - 1)
                        pe.matmul(ps_tr[:, 2 + s % 2, 0:2], cc("samebatch"), sums[:, s % 2, :],
                                  start=True, stop=True).then_inc(moments, 1)
            steps(pe, step)
            pe.wait_ge(fin_v, 1)
            for q in range(2):
                ins = pe.matmul(ps_tr[0:C, 0, q * BATCH:(q + 1) * BATCH], sums1c[:, q, :], cc("batchsum"), start=True,
                                stop=True)
            ins.then_inc(fin_p, 1)


def toeplitz(t, dy, b, y0, y1, x0, x1):
    off = PITCH * (2 * BR - 1 + BR * dy - y0) + BC * b + 3 * BC - 1 - x0
    return bass.AP(t.tensor, t.offset + off, [t.ap[0], [-PITCH, y1 - y0], [-1, x1 - x0]])


def window_pass(nc, x1, out, prm, const, gn2):
    B = NWIN
    LOAD, QKV, ATT, PROJ, MLPS = range(5)
    KD_DVE = 2
    with ExitStack() as ctx:
        def sb(name, shape, dtype=F32):
            return ctx.enter_context(nc.sbuf_tensor("b_" + name, shape, dtype))

        def sem(name):
            return ctx.enter_context(nc.semaphore(name))

        cst = sb("const", [P, NCONST])
        wraw = sb("wraw", [C, 3, C])
        woraw = sb("woraw", [C, C])
        w1raw = sb("w1raw", [C, MLP])
        wqk = sb("wqk", [C + 1, 2, P])
        wqkraw = sb("wqkraw", [C, 2, P])
        wv = sb("wv", [C, 2, C // 2])
        w1 = sb("w1s", [C, MLP])
        w2 = sb("w2s", [P, NM, C])
        w2_hi = sb("w2_hi", [P, NM, C], F32R)
        w2_lo = sb("w2_lo", [P, NM, C], F32R)
        centre = sb("centre", [C, C], F32R)
        cols = sb("cols", [P, 16])
        LN1S, LN1B, LN2S, LN2B, BV, BO, B2, B1, EPS, BVT = 0, 1, 2, 3, 4, 5, 6, 7, 10, 11
        xs = sb("xs", [C, B, WIN, XW])
        t0 = sb("t0", [C, B, NT])
        t0_hi = sb("t0_hi", [C, 2, NT], F32R)
        t0_lo = sb("t0_lo", [C, 2, NT], F32R)
        gnc = sb("gnc", [C, 2])
        sq = sb("sq", [C, NT])
        lg = sb("lg", [C, NT])
        rstd = sb("rstd", [C, NT])
        h1 = sb("h1", [C + 1, NT])
        h2 = sb("h2", [C, NT])
        q_hi = sb("q_hi", [P, 2, QG, PAIRS, P], F32R)
        q_lo = sb("q_lo", [P, 2, QG, PAIRS, P], F32R)
        k_hi = sb("k_hi", [P, QG * PAIRS, TOK], F32R)
        k_lo = sb("k_lo", [P, QG * PAIRS, TOK])
        kd_hi = sb("kd_hi", [P, 2, QG * PAIRS, HPG, TOK], F32R)
        kd_lo = sb("kd_lo", [P, 2, QG * PAIRS, HPG, TOK], F32R)
        vd = sb("vd", [P, 2, NWIN, HEADS // 2, 2, VA])
        mx = sb("mx", [P, 2, HEADS])
        ss = sb("ss", [P, 2, HEADS, TOK])
        probs = sb("probs", [P, 2, HEADS, WS])
        pt = sb("probs_t", [P, 2, HEADS // 2, 2, WS])
        rden = sb("rden", [P, PAIRS * HEADS])
        o = sb("o", [P, PAIRS, C])
        ot = sb("ot", [C, PAIRS, 2, TOK])
        t1 = sb("t1", [C, 2, NT])
        mid = sb("mid", [P, NM, NT])
        mid_hi = sb("mid_hi", [P, NM, NT], F32R)
        mid_lo = sb("mid_lo", [P, NM, NT], F32R)
        y = sb("y", [C, 2, NT])
        outs = sb("outs", [C, 2, WIN, XW])
        ps_s = ctx.enter_context(nc.psum_tensor("ps_s", [P, QG, 512], F32))
        ps_t = ctx.enter_context(nc.psum_tensor("ps_t", [P, 2, 512], F32))
        ps_pv = ctx.enter_context(nc.psum_tensor("ps_pv", [P, 512], F32))
        ps_xc = ctx.enter_context(nc.psum_tensor("ps_xc", [P, 512], F32))
        ps_ring = [ctx.enter_context(nc.psum_tensor(f"ps_ring{r}", [P, 512], F32)) for r in range(2)]

        x_loaded = [sem(f"xs_loaded{r}") for r in range(B)]
        stored = [sem(f"stored{r}") for r in range(2)]
        names = ("par_loaded zeroed_v zeroed_p wprep bias_ps bias_done gn_col wrapped t0_done t0_high t0_split mid_high mid_split xc1 sq1 var1 lg1 rstd1 "
                 "h1_done q_ps k_ps v_ps q_high k_high q_done k_done v_done kd_done kd_done_p s_ps mx_done sub_done exp_done t_ps pt_done "
                 "pv_ps rden_done o_done ot_ps ot_done wo_ps t1_done xc2 sq2 var2 lg2 rstd2 h2_done w1_ps gelu_done "
                 "w2_ps y_done added out_done").split()
        S = {n: sem("b_" + n) for n in names}

        def cc(name, rows=P):
            lo, hi = CONST[name]
            return cst[0:rows, lo:hi]

        def strip(i, s, off):
            n = B * i + s - off
            if isinstance(i, int) and not 0 <= n < BATCH * B:
                return None
            return n

        def steps(eng, step):
            for s in range(B):
                step(0, s)
            with eng.Fori(1, BATCH, 1) as i:
                for s in range(B):
                    step(i, s)
            for s in range(MLPS):
                step(BATCH, s)

        def after(eng, i, name, count):
            if not isinstance(i, int) or count > 0:
                eng.wait_ge(S[name], count)

        USES = [("w1a", MLPS, "gelu_done", 3, 1), ("w1b", MLPS, "gelu_done", 3, 2), ("w1c", MLPS, "gelu_done", 3, 3),
                ("ot", PROJ, "ot_done", 1, 1), ("var1", QKV, "lg1", 1, 1), ("wo", PROJ, "t1_done", 1, 1),
                ("q", QKV, "q_done", 1, 1), ("k", QKV, "k_done", 1, 1), ("v", QKV, "v_done", 1, 1),
                ("w2", MLPS, "y_done", 1, 1), ("var2", PROJ, "lg2", 1, 1)]
        NU = len(USES)

        def bank(s, use):
            u = [x[0] for x in USES].index(use)
            return ps_ring[(NU * s + u) % 2]

        def wait_bank(pe, i, s, use):
            u = NU * s + [x[0] for x in USES].index(use) - 2
            while True:
                _, off, name, per, nth = USES[u % NU]
                n = strip(i, u // NU, off)
                if n is not None:
                    pe.wait_ge(S[name], per * n + nth)
                    return
                u -= 2
                if isinstance(i, int) and B * i + u // NU < 0:
                    return

        def q_rows(t, s, w):
            return t[WS * w:WS * w + WS, (s - QKV) % 2, :, :, WS * w:WS * w + TOK].rearrange("p g n t -> p (g n) t")

        def tokens(t):
            return t[:, :, SHIFT:SHIFT + HW].rearrange("c y (w x) -> c w y x", x=WIN)

        def windows(t):
            return t.rearrange("c (w y x) -> c w y x", y=WIN, x=WIN)

        def rows(t, img, sl):
            r0 = SHIFT + WIN * sl
            parts = [(0, r0, min(WIN, HW - r0))]
            if r0 + WIN > HW:
                parts.append((HW - r0, 0, r0 + WIN - HW))
            im = t[bass.ds(img, 1), :, :, :].rearrange("b c h w -> c (b h) w")
            return [(d, n, im[:, r:r + n, :]) for d, r, n in parts]

        def settled(pool):
            pool.nop(nofuse=True)

        NPAR = 19
        block = ctx.enter_context(nc.Block())

        @block.sync
        def _(sp):
            def load(dst, src):
                sp.dma_start(dst, src).then_inc(S["par_loaded"], 16)
                count[0] += 1
            count = [0]
            sp.wait_ge(S["zeroed_v"], 1)
            load(cst[:, :], const)
            for j, n in enumerate(("wq", "wk", "wv")):
                load(wraw[:, j, :], prm[n])
            load(woraw[:, :], prm["wo"])
            load(w1raw[:, :], prm["w1"])
            load(w2[:, :, :], prm["w2"].rearrange("(m p) n -> p m n", p=P))
            for j, n in ((LN1S, "ln1_s"), (LN1B, "ln1_b"), (LN2S, "ln2_s"), (LN2B, "ln2_b"), (BV, "bv"), (BO, "bo"),
                         (B2, "b2")):
                load(cols[0:C, j:j + 1], prm[n].rearrange("(c a) -> c a", a=1))
            for j, n in enumerate(("bq", "bk")):
                load(wqk[C:C + 1, j, :].rearrange("c (g r) -> c g r", r=QR)[:, :, 0:GRP],
                     prm[n].rearrange("(a g r) -> a g r", a=1, g=QG))
            for m in range(NM):
                load(cols[:, B1 + m:B1 + m + 1], prm["b1"].rearrange("(m p a) -> m p a", p=P, a=1)[m])
            assert count[0] == NPAR, count

            def step(i, s):
                n = strip(i, s, LOAD)
                if n is not None:
                    after(sp, i, "out_done", n - B + 1)
                    for d, cnt, src in rows(x1, i, s):
                        sp.dma_start(xs[:, s, d:d + cnt, 0:HW], src).then_inc(x_loaded[s], 16)
                n = strip(i, s, MLPS)
                if n is not None:
                    sp.wait_ge(S["out_done"], n + 1)
                    sl = (s - MLPS) % B
                    for d, cnt, dst in rows(out, i + (s - MLPS) // B, sl):
                        sp.dma_start(dst, outs[:, sl % 2, d:d + cnt, 0:HW]).then_inc(stored[sl % 2], 16)
            steps(sp, step)
            sp.wait_ge(stored[0], 16 * BATCH * 4)
            sp.wait_ge(stored[1], 16 * BATCH * 5)

        @block.gpsimd
        def _(pool):
            for t in (q_hi, q_lo):
                ins = pool.memset(t[:, :, :, :, :].bitcast(F32), 0.0)
            ins.then_inc(S["zeroed_p"], 1)
            pool.memset(probs[:, :, :, :], 0.0).then_inc(S["zeroed_p"], 1)
            pool.memset(vd[:, :, :, :, :, :], 0.0).then_inc(S["zeroed_p"], 1)
            pool.wait_ge(S["zeroed_p"], 3)
            at = [(WS * half + lo, WS * half + hi, half) for half in range(2) for lo, hi in ((0, 32), (32, TOK))]
            for n, (lo, hi, half) in enumerate(at):
                pool.memset(vd[lo:hi, :, :, :, half, DH:VA], 1.0).then_inc(S["zeroed_p"], 1)
                pool.wait_ge(S["zeroed_p"], 4 + n)
            pool.memset(pt[:, :, :, :, :], 1.0).then_inc(S["zeroed_p"], 1)
            pool.wait_ge(S["par_loaded"], 16 * NPAR)

            def step(i, s):
                n = strip(i, s, LOAD)
                if n is not None:
                    if s == 0:
                        after(pool, i, "t0_done", n)
                        settled(pool)
                        pool.tensor_copy(gnc[:, :].unsqueeze(2), gn2[:, :, bass.ds(i, 1)]).then_inc(S["gn_col"], 1)
                        pool.wait_ge(S["gn_col"], i + 1)
                    pool.wait_ge(x_loaded[s], (16 if s < B - 1 else 32) * (i + 1))
                    settled(pool)
                    pool.tensor_copy(xs[:, s, :, HW:XW], xs[:, s, :, 0:SHIFT]).then_inc(S["wrapped"], 1)
                    pool.wait_ge(S["wrapped"], n + 1)
                    after(pool, i, "t1_done", n - B + 1)
                    settled(pool)
                    pool.tensor_scalar(windows(t0[:, s, :]), tokens(xs[:, s]), gnc[:, 0:1], gnc[:, 1:2], ALU.mult,
                                       ALU.add).then_inc(S["t0_done"], 1)
                    pool.wait_ge(S["t0_done"], n + 1)
                    after(pool, i, "xc1", n - 1)
                    settled(pool)
                    pool.tensor_scalar(t0_hi[:, s % 2, :], t0[:, s, :], 1.0, 0.0, ALU.mult, ALU.add).then_inc(
                        S["t0_high"], 1)
                    pool.wait_ge(S["t0_high"], n + 1)
                    settled(pool)
                    pool.tensor_tensor(t0_lo[:, s % 2, :], t0[:, s, :], t0_hi[:, s % 2, :].bitcast(F32),
                                       ALU.subtract).then_inc(S["t0_split"], 1)
                n = strip(i, s, MLPS)
                if n is not None:
                    for m in range(NM):
                        pool.wait_ge(S["gelu_done"], NM * n + m + 1)
                        after(pool, i, "w2_ps", n)
                        settled(pool)
                        pool.tensor_scalar(mid_hi[:, m, :], mid[:, m, :], 1.0, 0.0, ALU.mult, ALU.add).then_inc(
                            S["mid_high"], 1)
                        pool.wait_ge(S["mid_high"], NM * n + m + 1)
                        settled(pool)
                        pool.tensor_tensor(mid_lo[:, m, :], mid[:, m, :], mid_hi[:, m, :].bitcast(F32),
                                           ALU.subtract).then_inc(S["mid_split"], 1)
                n = strip(i, s, QKV)
                if n is not None:
                    pool.wait_ge(S["k_high"], n + 1)
                    after(pool, i, "s_ps", PAIRS * (n - 1))
                    settled(pool)
                    for j in range(KD_DVE, HPG):
                        ins = pool.tensor_scalar(kd_hi[:, (s - QKV) % 2, :, j, :], k_hi[:, :, :].bitcast(F32),
                                                 cc("headmask")[:, j:j + 1], 0.0, ALU.mult, ALU.add)
                    ins.then_inc(S["kd_done_p"], 1)
                n = strip(i, s, MLPS)
                if n is not None:
                    sl = (s - MLPS) % B
                    pool.wait_ge(S["y_done"], n + 1)
                    img = i + (s - MLPS) // B
                    before = img * (4 if sl % 2 == 0 else 5) + sl // 2
                    if not isinstance(i, int) or before > 0:
                        pool.wait_ge(stored[sl % 2], 16 * before)
                    settled(pool)
                    pool.tensor_tensor(tokens(outs[:, sl % 2]), windows(y[:, sl % 2, :]), tokens(xs[:, sl]),
                                       ALU.add).then_inc(S["added"], 1)
                    pool.wait_ge(S["added"], n + 1)
                    settled(pool)
                    pool.tensor_copy(outs[:, sl % 2, :, 0:SHIFT], outs[:, sl % 2, :, HW:XW]).then_inc(
                        S["out_done"], 1)
            steps(pool, step)

        @block.scalar
        def _(act):
            act.wait_ge(S["bias_done"], 2)
            act.wait_ge(S["zeroed_p"], 8)
            act.preload_act_table_set("natural_log_exp_and_others")

            def inv_std(n, var, var_ready, lg_done, r_done):
                act.wait_ge(S[var_ready], n + 1)
                act.activation(lg[:, :], var[0:C, 0:NT], ACT.Ln, bias=cols[0:C, EPS:EPS + 1]).then_inc(S[lg_done], 1)
                act.wait_ge(S[lg_done], n + 1)
                return act.activation(rstd[:, :], lg[:, :], ACT.Exp, scale=-0.5).then_inc(S[r_done], 1)

            def turned(i, m, p):
                if m is None:
                    return
                act.wait_ge(S["t_ps"], PAIRS * m + p + 1)
                after(act, i, "pv_ps", PAIRS * m + p - 1)
                act.activation(pt[:, p % 2, :, :, 0:TOK],
                               ps_t[:, :, :].rearrange("k a (b w t) -> k (a b) w t", b=4, w=2)[:, 0:HEADS // 2, :, 0:TOK],
                               ACT.Copy).then_inc(S["pt_done"], 1)

            def exps(i, m, p):
                if m is None:
                    return
                act.wait_ge(S["sub_done"], PAIRS * m + p + 1)
                after(act, i, "t_ps", PAIRS * m + p - 1)
                act.activation(probs[:, p % 2, :, 0:TOK], ss[:, p % 2, :, :], ACT.Exp,
                               scale=float(DH) ** -0.5).then_inc(S["exp_done"], 1)

            def square(n, src, done, scale=1.0):
                act.wait_ge(S[src], n + 1)
                return act.activation(sq[:, :], ps_xc[0:C, 0:NT], ACT.Square, scale=scale).then_inc(S[done], 1)

            def step(i, s):
                qkv, att, proj, mlps = (strip(i, s, x) for x in (QKV, ATT, PROJ, MLPS))
                turned(i, proj, PAIRS - 1)
                if qkv is not None:
                    after(act, i, "var2", qkv - (PROJ - QKV))
                    square(qkv, "xc1", "sq1", 1.0 / C)
                exps(i, att, 0)
                act.preload_act_table_set("gelu_apprx_tanh_and_others")
                if mlps is not None:
                    for m, use in enumerate(("w1a", "w1b", "w1c")):
                        if m == NM - 1:
                            turned(i, att, 0)
                        act.wait_ge(S["w1_ps"], NM * mlps + m + 1)
                        after(act, i, "mid_split", NM * (mlps - 1) + m + 1)
                        act.activation(mid[:, m, :], bank(s, use)[:, 0:NT], ACT.Gelu_apprx_tanh,
                                       bias=cols[:, B1 + m:B1 + m + 1]).then_inc(S["gelu_done"], 1)
                if mlps is None:
                    turned(i, att, 0)
                act.preload_act_table_set("natural_log_exp_and_others")
                exps(i, att, 1)
                if qkv is not None:
                    after(act, i, "h2_done", qkv - (PROJ - QKV))
                    inv_std(qkv, bank(s, "var1"), "var1", "lg1", "rstd1")
                turned(i, att, 1)
                if qkv is not None:
                    act.wait_ge(S["q_ps"], qkv + 1)
                    after(act, i, "s_ps", PAIRS * (qkv - 1))
                    for w in range(2):
                        ins = act.activation(q_rows(q_hi, s, w), bank(s, "q")[WS * w:WS * w + WS, 0:NT].rearrange(
                            "p (n t) -> p n t", t=TOK), ACT.Copy)
                    ins.then_inc(S["q_high"], 1)
                    act.wait_ge(S["k_ps"], qkv + 1)
                    after(act, i, "kd_done", qkv)
                    after(act, i, "kd_done_p", qkv)
                    act.activation(k_hi[:, :, :], bank(s, "k")[:, 0:NT].rearrange("p (n t) -> p n t", t=TOK),
                                   ACT.Copy).then_inc(S["k_high"], 1)
                exps(i, att, 2)
                if proj is not None:
                    act.wait_ge(S["var1"], qkv + 1 if qkv is not None else BATCH * B)
                    square(proj, "xc2", "sq2")
                turned(i, att, 2)
                exps(i, att, 3)
                if proj is not None:
                    act.wait_ge(S["h1_done"], qkv + 1 if qkv is not None else BATCH * B)
                    inv_std(proj, bank(s, "var2"), "var2", "lg2", "rstd2")
            steps(act, step)

        @block.vector
        def _(dve):
            dve.memset(wqkraw[:, :, :], 0.0)
            dve.memset(h1[:, :], 1.0)
            dve.memset(wqk[:, :, :], 0.0)
            dve.memset(cols[:, :], 0.0).then_inc(S["zeroed_v"], 1)
            dve.wait_ge(S["par_loaded"], 16 * NPAR)
            dve.memset(cols[:, EPS:EPS + 1], 1e-6)
            for j in range(2):
                ins = dve.tensor_copy(wqkraw[:, j, :].rearrange("c (g r) -> c g r", r=QR)[:, :, 0:GRP],
                                      wraw[:, j, :].rearrange("c (g r) -> c g r", r=GRP))
            ins.then_inc(S["wprep"], 1)
            dve.wait_ge(S["wprep"], 1)
            for j in range(2):
                dve.tensor_scalar(wqk[0:C, j, :], wqkraw[:, j, :], cols[0:C, LN1S:LN1S + 1], None, ALU.mult)
            for a in range(2):
                dve.tensor_scalar(wv[:, a, :].rearrange("c (h d) -> c h d", d=DH),
                                  wraw[:, 2, :].rearrange("c (h a d) -> c h a d", a=2, d=DH)[:, :, a, :],
                                  cols[0:C, LN1S:LN1S + 1], None, ALU.mult)
            dve.tensor_scalar(w1[:, :], w1raw[:, :], cols[0:C, LN2S:LN2S + 1], None, ALU.mult).then_inc(S["wprep"], 1)
            dve.tensor_copy(centre[:, :], cc("centre_c", C))
            dve.tensor_copy(w2_hi[:, :, :], w2[:, :, :]).then_inc(S["wprep"], 1)
            dve.wait_ge(S["wprep"], 3)
            dve.tensor_tensor(w2_lo[:, :, :], w2[:, :, :], w2_hi[:, :, :].bitcast(F32), ALU.subtract).then_inc(
                S["wprep"], 1)
            dve.wait_ge(S["bias_ps"], 1)
            dve.tensor_tensor(wqk[C:C + 1, :, :], wqk[C:C + 1, :, :],
                              ps_xc[C:C + 1, P:3 * P].rearrange("p (j c) -> p j c", j=2), ALU.add)
            dve.tensor_tensor(cols[:, B1:B1 + NM], cols[:, B1:B1 + NM], ps_xc[:, 4:4 + NM], ALU.add)
            dve.tensor_tensor(cols[0:C, BVT:BVT + 1], cols[0:C, BV:BV + 1], ps_xc[0:C, 2:3], ALU.add).then_inc(
                S["bias_done"], 1)
            dve.wait_ge(S["bias_ps"], 2)
            dve.tensor_tensor(cols[0:C, BO:BO + 1], cols[0:C, BO:BO + 1], ps_pv[0:C, 0:1], ALU.add).then_inc(
                S["bias_done"], 1)
            dve.wait_ge(S["bias_done"], 2)
            dve.wait_ge(S["zeroed_p"], 8)

            def shift_scores(i, m, p):
                if m is None:
                    return
                scores = ps_s[:, :, 0:HPG * TOK].rearrange("q g (j t) -> q g j t", j=HPG)
                dve.wait_ge(S["s_ps"], PAIRS * m + p + 1)
                dve.tensor_reduce(mx[:, p % 2, :].rearrange("q (g j) -> q g j", g=QG), scores, AX.X,
                                  ALU.max).then_inc(S["mx_done"], 1)
                dve.wait_ge(S["mx_done"], PAIRS * m + p + 1)
                after(dve, i, "exp_done", PAIRS * m + p - 1)
                dve.tensor_tensor(ss[:, p % 2, :, :].rearrange("q (g j) t -> q g j t", g=QG), scores,
                                  mx[:, p % 2, :].rearrange("q (g j) -> q g j", g=QG).unsqueeze(3).broadcast_to(
                                      (P, QG, HPG, TOK)), ALU.subtract).then_inc(S["sub_done"], 1)

            def step(i, s):
                qkv, att, proj, mlps = (strip(i, s, x) for x in (QKV, ATT, PROJ, MLPS))
                shift_scores(i, att, 0)
                if proj is not None:
                    pv = ps_pv[:, 0:PAIRS * HEADS * VA].rearrange("q (n d) -> q n d", d=VA)
                    dve.wait_ge(S["pv_ps"], PAIRS * (proj + 1))
                    dve.reciprocal(rden[:, :].unsqueeze(2), pv[:, :, DH:VA]).then_inc(S["rden_done"], 1)
                    dve.wait_ge(S["rden_done"], proj + 1)
                    after(dve, i, "ot_ps", proj)
                    dve.tensor_tensor(o[:, :, :].rearrange("q p (h d) -> q (p h) d", d=DH), pv[:, :, 0:DH],
                                      rden[:, :].unsqueeze(2).broadcast_to((P, PAIRS * HEADS, DH)),
                                      ALU.mult).then_inc(S["o_done"], 1)
                shift_scores(i, att, 1)
                if proj is not None:
                    dve.wait_ge(S["ot_ps"], proj + 1)
                    after(dve, i, "wo_ps", proj)
                    dve.tensor_copy(ot[:, :, :, :], bank(s, "ot")[0:C, :].rearrange("c (p w t) -> c p w t", p=PAIRS, w=2)[
                        :, :, :, 0:TOK]).then_inc(S["ot_done"], 1)
                if qkv is not None:
                    dve.wait_ge(S["rstd1"], qkv + 1)
                    after(dve, i, "v_ps", qkv)
                    dve.scalar_tensor_tensor(h1[0:C, :], ps_xc[0:C, 0:NT], 1.0 / C, rstd[:, :], ALU.mult,
                                             ALU.mult).then_inc(S["h1_done"], 1)
                if proj is not None:
                    dve.wait_ge(S["wo_ps"], proj + 1)
                    after(dve, i, "y_done", proj - 1)
                    dve.scalar_tensor_tensor(t1[:, (s - PROJ) % 2, :], bank(s, "wo")[0:C, 0:NT], cols[0:C, BO:BO + 1],
                                             t0[:, (s - PROJ) % B, :], ALU.add, ALU.add).then_inc(S["t1_done"], 1)
                shift_scores(i, att, 2)
                if qkv is not None:
                    dve.wait_ge(S["q_high"], qkv + 1)
                    after(dve, i, "s_ps", PAIRS * (qkv - 1))
                    for w in range(2):
                        ins = dve.tensor_tensor(q_rows(q_lo, s, w), bank(s, "q")[WS * w:WS * w + WS, 0:NT].rearrange(
                            "p (n t) -> p n t", t=TOK), q_rows(q_hi, s, w).bitcast(F32), ALU.subtract)
                    ins.then_inc(S["q_done"], 1)
                    dve.wait_ge(S["k_high"], qkv + 1)
                    after(dve, i, "kd_done", qkv)
                    dve.tensor_tensor(k_lo[:, :, :], bank(s, "k")[:, 0:NT].rearrange("p (n t) -> p n t", t=TOK),
                                      k_hi[:, :, :].bitcast(F32), ALU.subtract).then_inc(S["k_done"], 1)
                    for j in range(KD_DVE):
                        dve.tensor_scalar(kd_hi[:, (s - QKV) % 2, :, j, :], k_hi[:, :, :].bitcast(F32),
                                          cc("headmask")[:, j:j + 1], None, ALU.mult)
                shift_scores(i, att, 3)
                if qkv is not None:
                    sl = (s - QKV) % 2
                    dve.wait_ge(S["v_ps"], qkv + 1)
                    after(dve, i, "pv_ps", PAIRS * (qkv - 1))
                    for a in range(2):
                        r = slice(WS * a, WS * a + TOK)
                        ins = dve.tensor_copy(vd[r, sl, :, :, a, 0:DH],
                                              bank(s, "v")[r, 0:NWIN * C // 2].rearrange("t (w h d) -> t w h d", w=NWIN,
                                                                                         d=DH))
                    ins.then_inc(S["v_done"], 1)
                    dve.wait_ge(S["k_done"], qkv + 1)
                    for j in range(HPG):
                        ins = dve.tensor_scalar(kd_lo[:, sl, :, j, :], k_lo[:, :, :], cc("headmask")[:, j:j + 1], None,
                                                ALU.mult)
                    ins.then_inc(S["kd_done"], 1)
                if mlps is not None:
                    dve.wait_ge(S["w2_ps"], mlps + 1)
                    after(dve, i, "added", mlps - 1)
                    dve.scalar_tensor_tensor(y[:, (s - MLPS) % 2, :], bank(s, "w2")[0:C, 0:NT], cols[0:C, B2:B2 + 1],
                                             t1[:, (s - MLPS) % 2, :], ALU.add, ALU.add).then_inc(S["y_done"], 1)
                if proj is not None:
                    dve.wait_ge(S["rstd2"], proj + 1)
                    after(dve, i, "w1_ps", NM * proj)
                    dve.tensor_tensor(h2[:, :], ps_xc[0:C, 0:NT], rstd[:, :], ALU.mult).then_inc(S["h2_done"], 1)
            steps(dve, step)

        @block.tensor
        def _(pe):
            pe.wait_ge(S["wprep"], 4)
            pe.matmul(ps_xc[C:C + 1, P:3 * P], cols[0:C, LN1B:LN1B + 1], wqkraw[:, :, :].rearrange("c j n -> c (j n)"),
                      start=True, stop=True, skip_group_check=True)
            for m in range(NM):
                pe.matmul(ps_xc[:, 4 + m:5 + m], w1raw[:, m * P:(m + 1) * P], cols[0:C, LN2B:LN2B + 1], start=True,
                          stop=True, skip_group_check=True)
            pe.matmul(ps_xc[0:C, 2:3], wraw[:, 2, :], cols[0:C, LN1B:LN1B + 1], start=True, stop=True,
                      skip_group_check=True).then_inc(S["bias_ps"], 1)
            pe.wait_ge(S["bias_done"], 1)
            pe.matmul(ps_pv[0:C, 0:1], woraw[:, :], cols[0:C, BVT:BVT + 1], start=True, stop=True).then_inc(
                S["bias_ps"], 1)
            pe.wait_ge(S["bias_done"], 2)
            pe.wait_ge(S["zeroed_p"], 8)

            def product(i, s, use, w, src, rows, done):
                wait_bank(pe, i, s, use)
                pe.matmul(bank(s, use)[0:rows, 0:NT], w, src, start=True, stop=True).then_inc(S[done], 1)

            def scores(i, s, m, p):
                if m is None:
                    return
                if p == 0:
                    for name in ("q_done", "kd_done", "kd_done_p"):
                        pe.wait_ge(S[name], m + 1)
                after(pe, i, "sub_done", PAIRS * m + p)
                par = (s - ATT) % 2
                for g in range(QG):
                    for n, (qs, ks) in enumerate(((q_hi, kd_hi), (q_hi, kd_lo), (q_lo, kd_hi))):
                        ins = pe.matmul(ps_s[:, g, 0:HPG * TOK], qs[:, par, g, p, :],
                                        ks[:, par, PAIRS * g + p, :, :].rearrange("p j t -> p (j t)"), start=(n == 0),
                                        stop=(n == 2))
                ins.then_inc(S["s_ps"], 1)

            def turn(i, m, p):
                if m is None:
                    return
                pe.wait_ge(S["exp_done"], PAIRS * m + p + 1)
                after(pe, i, "pt_done", PAIRS * m + p)
                for h in range(HEADS // 2):
                    ins = pe.transpose(ps_t[:, h // 4, (h % 4) * P:(h % 4 + 1) * P],
                                       probs[:, p % 2, 2 * h:2 * h + 2, :].rearrange("q h t -> q (h t)"), cc("ident"))
                ins.then_inc(S["t_ps"], 1)

            def times_v(i, par, m, p):
                if m is None:
                    return
                if p == 0:
                    pe.wait_ge(S["v_done"], m + 1)
                    after(pe, i, "o_done", m)
                pe.wait_ge(S["pt_done"], PAIRS * m + p + 1)
                for h in range(HEADS // 2):
                    for w in range(2):
                        col = (p * HEADS + 2 * h) * VA
                        ins = pe.matmul(ps_pv[WS * w:WS * w + WS, col:col + 2 * VA], pt[:, p % 2, h, w, :],
                                        vd[:, par, 2 * p + w, h, :, :].rearrange("k a d -> k (a d)"), start=True,
                                        stop=True, skip_group_check=True)
                ins.then_inc(S["pv_ps"], 1)

            def step(i, s):
                qkv, att, proj, mlps = (strip(i, s, x) for x in (QKV, ATT, PROJ, MLPS))
                scores(i, s, att, 0)
                turn(i, proj, PAIRS - 1)
                if qkv is not None:
                    pe.wait_ge(S["t0_split"], qkv + 1)
                    after(pe, i, "h2_done", qkv - (PROJ - QKV))
                    pe.matmul(ps_xc[0:C, 0:NT], centre[:, :], t0_hi[:, (s - QKV) % 2, :], start=True, stop=False)
                    pe.matmul(ps_xc[0:C, 0:NT], centre[:, :], t0_lo[:, (s - QKV) % 2, :], start=False,
                              stop=True).then_inc(S["xc1"], 1)
                if mlps is not None:
                    pe.wait_ge(S["h2_done"], mlps + 1)
                    product(i, s, "w1a", w1[:, 0:P], h2[:, :], P, "w1_ps")
                    product(i, s, "w1b", w1[:, P:2 * P], h2[:, :], P, "w1_ps")
                times_v(i, (s - PROJ) % 2, proj, PAIRS - 1)

                scores(i, s, att, 1)
                turn(i, att, 0)
                if mlps is not None:
                    product(i, s, "w1c", w1[:, 2 * P:3 * P], h2[:, :], P, "w1_ps")
                if proj is not None:
                    pe.wait_ge(S["o_done"], proj + 1)
                    wait_bank(pe, i, s, "ot")
                    for p in range(PAIRS):
                        ins = pe.transpose(bank(s, "ot")[0:C, p * P:(p + 1) * P], o[:, p, :], cc("ident"))
                    ins.then_inc(S["ot_ps"], 1)
                times_v(i, (s - ATT) % 2, att, 0)
                if qkv is not None:
                    pe.wait_ge(S["sq1"], qkv + 1)
                    product(i, s, "var1", cc("average", C), sq[:, :], C, "var1")

                scores(i, s, att, 2)
                turn(i, att, 1)
                if proj is not None:
                    pe.wait_ge(S["ot_done"], proj + 1)
                    product(i, s, "wo", woraw[:, :], ot[:, :, :, :].rearrange("c p w t -> c (p w t)"), C, "wo_ps")
                if qkv is not None:
                    pe.wait_ge(S["h1_done"], qkv + 1)
                    for j, name in enumerate("qk"):
                        wait_bank(pe, i, s, name)
                        pe.nop(nofuse=True)
                        for g in range(QG):
                            for w in range(2):
                                ins = pe.matmul(
                                    bank(s, name)[WS * w:WS * w + WS, g * NT // 2:(g + 1) * NT // 2],
                                    wqk[:, j, QR * g:QR * g + QR],
                                    h1[:, :].rearrange("c (p w t) -> c p w t", w=2, t=TOK)[:, :, w, :],
                                    start=True, stop=True, skip_group_check=True)
                        ins.then_inc(S[name + "_ps"], 1)
                if proj is not None:
                    pe.wait_ge(S["t1_done"], proj + 1)
                    pe.wait_ge(S["h1_done"], qkv + 1 if qkv is not None else BATCH * B)
                    pe.matmul(ps_xc[0:C, 0:NT], cc("center", C), t1[:, (s - PROJ) % 2, :], start=True,
                              stop=True).then_inc(S["xc2"], 1)
                times_v(i, (s - ATT) % 2, att, 1)

                scores(i, s, att, 3)
                turn(i, att, 2)
                if qkv is not None:
                    wait_bank(pe, i, s, "v")
                    for w in range(NWIN):
                        for a in range(2):
                            ins = pe.matmul(bank(s, "v")[WS * a:WS * a + TOK, w * C // 2:(w + 1) * C // 2],
                                            h1[0:C, w * TOK:(w + 1) * TOK], wv[:, a, :], start=True, stop=True,
                                            skip_group_check=True)
                    ins.then_inc(S["v_ps"], 1)
                if mlps is not None:
                    wait_bank(pe, i, s, "w2")
                    for m in range(NM):
                        pe.wait_ge(S["mid_split"], NM * mlps + m + 1)
                        for n, (w, src) in enumerate(((w2_hi, mid_hi), (w2_lo, mid_hi), (w2_hi, mid_lo))):
                            ins = pe.matmul(bank(s, "w2")[0:C, 0:NT], w[:, m, :], src[:, m, :],
                                            start=(m == 0 and n == 0), stop=(m == NM - 1 and n == 2))
                    ins.then_inc(S["w2_ps"], 1)
                if proj is not None:
                    pe.wait_ge(S["sq2"], proj + 1)
                    product(i, s, "var2", cc("average", C), sq[:, :], C, "var2")
                times_v(i, (s - ATT) % 2, att, 2)
            steps(pe, step)


PARAMS = ("ln1_s", "ln1_b", "wq", "bq", "wk", "bk", "wv", "bv", "wo", "bo", "ln2_s", "ln2_b", "w1", "b1", "w2", "b2")


def build(nc, x, weight, conv_bias, prm, const, out):
    wpad = nc.dram_tensor("filters_padded", [C, WLEN], F32, kind="Internal").ap()
    x1 = nc.dram_tensor("x1_scratch", [BATCH, C, HW, HW], F32, kind="Internal").ap()
    with nc.sbuf_tensor("gn2", [C, 2, BATCH], F32) as gn2:
        conv_pass(nc, x, weight, conv_bias, const, wpad, x1, gn2)
        window_pass(nc, x1, out, prm, const, gn2)


def kernel(**inputs):
    import concourse.bacc as bacc
    from concourse.bass_utils import run_bass_kernel_spmd

    nc = bacc.Bacc("TRN2", target_bir_lowering=False, num_devices=1)
    arrays = {}

    def given(name, a):
        arrays[name] = np.ascontiguousarray(a)
        return nc.dram_tensor(name, arrays[name].shape, F32, kind="ExternalInput").ap()
    x = given("x", inputs["x"])
    weight = given("conv_weight", inputs["L0_conv_weight"])
    conv_bias = given("conv_bias", inputs["L0_conv_bias_term"])
    prm = {n: given(n, inputs["L1_conv_" + n]) for n in PARAMS}
    const = given("constants", constants())
    out = nc.dram_tensor("out", (BATCH, C, HW, HW), F32, kind="ExternalOutput").ap()
    build(nc, x, weight, conv_bias, prm, const, out)
    return run_bass_kernel_spmd(nc, [arrays], core_ids=[0]).results[0]["out"]
```
